# Optimizing a Trainium2 kernel written in Bass

```python
import numpy as np
import jax
import jax.numpy as jnp

def _softmax(x, axis=-1):
    return jax.nn.softmax(x, axis=axis)

def _gelu(x):
    return jax.nn.gelu(x, approximate=True)

def _silu(x):
    return jax.nn.silu(x)

def _sigmoid(x):
    return jax.nn.sigmoid(x)

def _layernorm(x, axis=-1, eps=1e-05):
    m = jnp.mean(x, axis=axis, keepdims=True)
    v = jnp.var(x, axis=axis, keepdims=True)
    return (x - m) / jnp.sqrt(v + eps)

def _scatter_add(tgt, idx, src, axis=0):
    return tgt.at[idx].add(src)

def _segment_sum(src, seg, n):
    return jax.ops.segment_sum(src, seg, n)
kernel_name = 'mk_adaln_ffn_d1_seqx_r2_eaa03c'

def setup_inputs(seed: int=0):
    np.random.seed(seed)
    _w = jnp.asarray

    def _rec_inputs():
        import jax
        import jax.numpy as jnp
        _rk = jax.random.key(seed)
        x = 0.0001734 + 0.8201 * jax.random.normal(jax.random.fold_in(_rk, 1), (32, 128, 2048), jnp.float32)
        _lenS = 128 - jax.random.randint(jax.random.fold_in(_rk, 7), (32,), 0, max(1, 128 // 4) + 1, jnp.int32)
        _lenS2 = 128 - jax.random.randint(jax.random.fold_in(_rk, 8), (32,), 0, max(1, 128 // 4) + 1, jnp.int32)
        itok_B_0_7 = jax.random.randint(jax.random.fold_in(_rk, 11), (32,), 0, 8, jnp.int32)
        itok_B_2182_4065 = jax.random.randint(jax.random.fold_in(_rk, 13), (32,), 1091, 2033, jnp.int32)
        return (x, itok_B_0_7, itok_B_2182_4065, _lenS)
    x, itok_B_0_7, itok_B_2182_4065, _lenS = _rec_inputs()

    def _L0_cond_setup():
        import jax, jax.numpy as jnp
        import numpy as np
        SESSION_CHANNELS = [128, 160, 192, 224, 240, 248, 252, 128]
        N_SESS = len(SESSION_CHANNELS)
        B, MAX_C, MAX_T = (16, 128, 2048)
        HID, N_SRC = (256, 128)
        key = jax.random.key(seed)
        ks = jax.random.split(key, 7)
        session_ids = jax.random.randint(ks[0], (B,), 0, N_SESS)
        chan_table = jnp.asarray(SESSION_CHANNELS)
        channel_counts = chan_table[session_ids]
        seq_lens = jax.random.randint(ks[1], (B,), MAX_T // 2, MAX_T + 1)
        x = jax.random.normal(ks[2], (B, MAX_C, MAX_T), jnp.float32)
        cmask = (jnp.arange(MAX_C)[None, :] < channel_counts[:, None]).astype(x.dtype)
        tmask = (jnp.arange(MAX_T)[None, :] < seq_lens[:, None]).astype(x.dtype)
        x = x * cmask[:, :, None] * tmask[:, None, :]
        lim1 = 1.0 / np.sqrt(MAX_C)
        W_sess = jax.random.uniform(ks[3], (N_SESS, MAX_C, HID), jnp.float32, -lim1, lim1)
        b_sess = jax.random.uniform(ks[4], (N_SESS, HID), jnp.float32, -lim1, lim1)
        lim2 = 1.0 / np.sqrt(HID)
        W2 = jax.random.uniform(ks[5], (HID, N_SRC), jnp.float32, -lim2, lim2)
        b2 = jax.random.uniform(ks[6], (N_SRC,), jnp.float32, -lim2, lim2)
        return dict(x=x, session_ids=session_ids, channel_counts=channel_counts, seq_lens=seq_lens, W_sess=W_sess, b_sess=b_sess, W2=W2, b2=b2)
    _L0_cond_all = _L0_cond_setup()
    _L0_cond_in = {k: v for k, v in _L0_cond_all.items() if k in ('W_sess', 'b_sess', 'W2', 'b2')}
    del _L0_cond_all

    def _L0_ffn_setup():
        import jax, jax.numpy as jnp
        import numpy as np
        E4M3_MAX = 448.0
        E5M2_MAX = 57344.0
        EPS = 1e-12
        IN_FEATURES = 2048
        OUT_FEATURES = 2048
        BATCH, SEQ = (1, 1024)

        def _amax_to_scale(amax, fp8_max):
            return fp8_max / jnp.maximum(amax, EPS)

        def _to_fp8_saturated(t, fp8_max, fp8_dtype):
            return jnp.clip(t, -fp8_max, fp8_max).astype(fp8_dtype)
        key = jax.random.key(seed)
        kx, kw, kb = jax.random.split(key, 3)
        x = jax.random.normal(kx, (BATCH, SEQ, IN_FEATURES), dtype=jnp.float32)
        weight = jax.random.normal(kw, (OUT_FEATURES, IN_FEATURES), dtype=jnp.float32) * 0.02
        bias = jax.random.normal(kb, (OUT_FEATURES,), dtype=jnp.float32) * 0.02
        return {'x': x, 'weight': weight, 'bias': bias}
    _L0_ffn_all = _L0_ffn_setup()
    _L0_ffn_in = {k: v for k, v in _L0_ffn_all.items() if k in ('weight', 'bias')}
    del _L0_ffn_all
    return {'x': x, 'itok_B_0_7': itok_B_0_7, 'itok_B_2182_4065': itok_B_2182_4065, '_lenS': _lenS, 'L0_cond_W_sess': _L0_cond_in['W_sess'], 'L0_cond_b_sess': _L0_cond_in['b_sess'], 'L0_cond_W2': _L0_cond_in['W2'], 'L0_cond_b2': _L0_cond_in['b2'], 'L0_ffn_weight': _L0_ffn_in['weight'], 'L0_ffn_bias': _L0_ffn_in['bias']}

def reference(x, itok_B_0_7, itok_B_2182_4065, _lenS, L0_cond_W_sess, L0_cond_b_sess, L0_cond_W2, L0_cond_b2, L0_ffn_weight, L0_ffn_bias):
    import jax
    import jax.numpy as jnp

    def _L0_cond_ref(x, session_ids, channel_counts, seq_lens, W_sess, b_sess, W2, b2):
        import jax, jax.numpy as jnp
        import numpy as np
        SESSION_CHANNELS = [128, 160, 192, 224, 240, 248, 252, 128]
        N_SESS = len(SESSION_CHANNELS)
        B, MAX_C, MAX_T = (16, 128, 2048)
        HID, N_SRC = (256, 128)
        cmask = (jnp.arange(x.shape[1])[None, :] < channel_counts[:, None]).astype(x.dtype)
        xm = x * cmask[:, :, None]
        W = W_sess[session_ids]
        b = b_sess[session_ids]
        h = jnp.einsum('bct,bch->bht', xm, W) + b[:, :, None]
        h = jax.nn.gelu(h, approximate=False)
        out = jnp.einsum('bht,hs->bst', h, W2) + b2[None, :, None]
        tmask = (jnp.arange(x.shape[2])[None, :] < seq_lens[:, None]).astype(x.dtype)
        return out * tmask[:, None, :]

    def _L0_ffn_ref(x, weight, bias):
        import jax, jax.numpy as jnp
        import numpy as np
        E4M3_MAX = 448.0
        E5M2_MAX = 57344.0
        EPS = 1e-12
        IN_FEATURES = 2048
        OUT_FEATURES = 2048
        BATCH, SEQ = (1, 1024)

        def _amax_to_scale(amax, fp8_max):
            return fp8_max / jnp.maximum(amax, EPS)

        def _to_fp8_saturated(t, fp8_max, fp8_dtype):
            return jnp.clip(t, -fp8_max, fp8_max).astype(fp8_dtype)
        w_amax = jnp.max(jnp.abs(weight))
        w_scale = _amax_to_scale(w_amax, E4M3_MAX)
        w_q = _to_fp8_saturated(weight * w_scale, E4M3_MAX, jnp.float8_e4m3fn)
        x_amax = jnp.max(jnp.abs(x))
        x_scale = _amax_to_scale(x_amax, E5M2_MAX)
        x_q = _to_fp8_saturated(x * x_scale, E5M2_MAX, jnp.float8_e5m2)
        acc = jnp.einsum('bsk,nk->bsn', x_q.astype(jnp.float32), w_q.astype(jnp.float32))
        out = acc * (1.0 / x_scale) * (1.0 / w_scale) + bias
        return out
    x = x + _L0_ffn_ref(_L0_cond_ref(x, itok_B_0_7, _lenS, itok_B_2182_4065, L0_cond_W_sess, L0_cond_b_sess, L0_cond_W2, L0_cond_b2), L0_ffn_weight, L0_ffn_bias)
    return x

_drawn_inputs = setup_inputs


def setup_inputs(seed=0):
    import zlib

    import numpy as np

    out = dict(_drawn_inputs(seed))
    spreads = {}
    factors = {'L0_cond_b_sess': 3.075}
    for name, (base, spread) in spreads.items():
        noise = np.random.default_rng([zlib.crc32(name.encode()), seed]).standard_normal(out[name].shape)
        drawn = base * np.exp(spread * noise) if base else spread * noise
        out[name] = jnp.asarray(drawn.astype(out[name].dtype))
    for name, factor in factors.items():
        out[name] = (out[name] * factor).astype(out[name].dtype)
    return out
```

```python
import concourse.bass as bass
from concourse import mybir
from contextlib import ExitStack
import numpy as np


def adaln_ffn(nc, x, ids, lens, counts, w_sess, b_sess, w2, b2, weight, bias, out, masked_out):
    fp32, bf16, fp8, i32 = mybir.dt.float32, mybir.dt.bfloat16, mybir.dt.float8e5, mybir.dt.int32
    ALU, ACT, AX = mybir.AluOpType, mybir.ActivationFunctionType, mybir.AxisListType
    ds = bass.ds

    P = 128
    B, C, T = x.shape
    NSESS, _, HID = w_sess.shape
    HT = HID // P
    F = weight.shape[0]
    BANK = 512
    UNIT = 2 * BANK
    UPB = T // UNIT
    NT = F // P
    KT = T // P
    NC = F // BANK
    GT = KT // NC
    STEPS = B // 2
    E4M3_MAX, E5M2_MAX, EPS = 448.0, 57344.0, 1e-12
    EXPONENT = 0x7F800000
    E4M3_MIN_NORMAL = 2.0 ** -6
    ROUND_AT = 1.5 * 2.0 ** 20
    assert C == P and UPB == 2 and NT == KT and B == 2 * NT

    SCAN = NT // 4
    QUANT = SCAN + NT // 2
    SEGMENTS = [(0, SCAN, True, False, False), (SCAN, SCAN + 1, False, True, False),
                (SCAN + 1, QUANT, False, True, True), (QUANT, QUANT + 1, False, False, True),
                (QUANT + 1, STEPS - 1, False, False, False), (STEPS - 1, STEPS, False, False, False)]
    FREE2, FREE4 = 2, 4
    ONE, DMA = 1, 16

    with ExitStack() as ctx:
        def sb(name, shape, dt):
            return ctx.enter_context(nc.sbuf_tensor(name, shape, dt))

        def sem(name):
            return ctx.enter_context(nc.semaphore(name))

        ids_i = sb("ids_i", [P, B], i32)
        counts_i = sb("counts_i", [P, B], i32)
        lens_i = sb("lens_i", [P, B], i32)
        ids_f = sb("ids_f", [P, B], fp32)
        counts_f = sb("counts_f", [P, B], fp32)
        lens_f = sb("lens_f", [P, B], fp32)
        chan = sb("chan", [P, 1], fp32)
        time = sb("time", [P, T], fp32)
        onehot = sb("onehot", [NSESS, B], fp32)
        cmask = sb("cmask", [P, B], fp32)
        bs_sb = sb("bs_sb", [NSESS, HID], fp32)
        hbias = sb("hbias", [P, HT, B], fp32)
        w2_sb = sb("w2_sb", [P, HT, P], fp32)
        b2_sb = sb("b2_sb", [P, 1], fp32)
        bias_sb = sb("bias_sb", [P, F], fp32)
        ident = sb("ident", [P, P], bf16)
        wqT = sb("wqT", [P, KT, F], bf16)
        w_max = sb("w_max", [P, NT], fp32)
        o_max = sb("o_max", [P, B * UPB], fp32)
        scales = sb("scales", [P, 12], fp32)
        w_pmax, w_amax, w_clip, w_rec, w_scale, w_inv = (scales[:, k:k + 1] for k in range(6))
        o_pmax, o_amax, o_rec, o_scale, o_inv, y_scale = (scales[:, k:k + 1] for k in range(6, 12))

        x_sb = sb("x_sb", [P, 2, T], fp32)
        wraw = sb("wraw", [P, 2, HID], fp32)
        wb = sb("wb", [P, 2, HID], fp32)
        h_sb = sb("h_sb", [P, 2, HT, UNIT], fp32)
        o_raw = sb("o_raw", [P, 2, UNIT], fp32)
        o_sb = sb("o_sb", [P, 2, T], fp32)
        wt = sb("wt", [P, 2, T], fp32)
        wv = sb("wv", [P, 2, T], fp32)
        wq = sb("wq", [P, T], bf16)
        q8 = sb("q8", [P, 2, T], fp8)
        qT = sb("qT", [P, 2, KT, P], bf16)
        v_sb = h_sb[:, 0, :, :].rearrange("p a n -> p (a n)")
        o_in, x2, y_sb = wt, wv, o_sb

        ps_h = ctx.enter_context(nc.psum_tensor("ps_h", [P, HT, UNIT], fp32))
        ps_o = ctx.enter_context(nc.psum_tensor("ps_o", [P, UNIT], fp32))
        ps_t = ctx.enter_context(nc.psum_tensor("ps_t", [P, 2, 2 * BANK], bf16))
        ps_y = [ps_h[:, n // 2, n % 2 * BANK:(n % 2 + 1) * BANK] for n in range(NC)]
        t_banks = [ps_o[:, 0:BANK], ps_o[:, BANK:UNIT],
                   ps_t[:, 0, :].bitcast(fp32), ps_t[:, 1, :].bitcast(fp32)]

        params_loaded = sem("params_loaded")
        ids_loaded = sem("ids_loaded")
        bias_loaded = sem("bias_loaded")
        iota_ready = sem("iota_ready")
        ident_zeroed = sem("ident_zeroed")
        ident_ready = sem("ident_ready")
        const_step = sem("const_step")
        onehot_ready = sem("onehot_ready")
        hbias_psum = sem("hbias_psum")
        hbias_ready = sem("hbias_ready")
        x_loaded = [sem(f"x_loaded{r}") for r in range(2)]
        wraw_loaded = [sem(f"wraw_loaded{r}") for r in range(2)]
        wb_ready = sem("wb_ready")
        h_psum_ready = sem("h_psum_ready")
        gelu_done = sem("gelu_done")
        o_psum_ready = sem("o_psum_ready")
        o_raw_ready = sem("o_raw_ready")
        o_masked = sem("o_masked")
        o_scanned = sem("o_scanned")
        o_stored = [sem(f"o_stored{r}") for r in range(2)]
        wt_loaded = [sem(f"wt_loaded{r}") for r in range(2)]
        wt_scanned = sem("wt_scanned")
        scale_step = sem("scale_step")
        w_pmax_ready = sem("w_pmax_ready")
        w_amax_ready = sem("w_amax_ready")
        w_scale_ready = sem("w_scale_ready")
        w_scaled = sem("w_scaled")
        w_exponent = sem("w_exponent")
        w_round_ready = sem("w_round_ready")
        w_added = sem("w_added")
        w_rounded = sem("w_rounded")
        w_transposed = sem("w_transposed")
        w_stored = sem("w_stored")
        o_pmax_ready = sem("o_pmax_ready")
        o_amax_ready = sem("o_amax_ready")
        o_in_loaded = [sem(f"o_in_loaded{r}") for r in range(2)]
        x2_loaded = [sem(f"x2_loaded{r}") for r in range(2)]
        xb_ready = sem("xb_ready")
        q_clipped = sem("q_clipped")
        q_ready = sem("q_ready")
        qT_psum = sem("qT_psum")
        qT_ready = sem("qT_ready")
        y_psum = sem("y_psum")
        y_ready = sem("y_ready")
        y_stored = [sem(f"y_stored{r}") for r in range(2)]

        gelu_turn = sem("gelu_turn")
        q_turn = sem("q_turn")
        transpose_turn = sem("transpose_turn")

        block = ctx.enter_context(nc.Block())

        def run_steps(eng, step):
            for first, end, scan, quant, trans in SEGMENTS:
                if end - first == 1:
                    step(first, scan, quant, trans, end == STEPS)
                else:
                    with eng.Fori(first, end) as i:
                        step(i, scan, quant, trans, False)

        @block.sync
        def _(sp):
            for r in range(2):
                sp.sem_inc(o_stored[r], DMA)
                sp.sem_inc(y_stored[r], DMA)
            for dst, src in ((ids_i, ids), (counts_i, counts), (lens_i, lens)):
                sp.dma_start(dst[:, :], src.partition_broadcast(P)).then_inc(ids_loaded, 16)
            sp.dma_start(bs_sb[:, :], b_sess).then_inc(params_loaded, 16)
            sp.dma_start(w2_sb[:, :, :], w2.rearrange("(j p) s -> p j s", p=P)).then_inc(params_loaded, 16)
            sp.dma_start(b2_sb[:, :], b2.rearrange("(p a) -> p a", a=1)).then_inc(params_loaded, 16)
            sp.wait_ge(ids_loaded, 48)

            def load_batch(b, r):
                sid = sp.value_load(ids_i[0:1, ds(b, 1)], min_val=0, max_val=NSESS - 1)
                sp.dma_start(wraw[:, r, :], w_sess[ds(sid, 1), :, :].rearrange("a c h -> (a c) h"))\
                  .then_inc(wraw_loaded[r], 16)
                sp.dma_start(x_sb[:, r, :], x[ds(b, 1), :, :].rearrange("a c t -> (a c) t"))\
                  .then_inc(x_loaded[r], 16)

            def load_weight(tile, r):
                sp.dma_start(wt[:, r, :], weight[ds(tile * P, P), :]).then_inc(wt_loaded[r], 16)

            load_batch(0, 0)
            load_batch(1, 1)
            sp.dma_start(bias_sb[:, :], bias.partition_broadcast(P)).then_inc(bias_loaded, 16)

            def step(i, scan, quant, trans, last):
                for r in range(2):
                    b = i * 2 + r
                    if scan:
                        for k in range(2):
                            sp.wait_ge(wt_scanned, b * 2 + k + 1)
                            load_weight(b * 2 + k, k)
                    if quant:
                        n = b - 2 * SCAN
                        sp.wait_ge(wt_scanned, NT + FREE2)
                        sp.wait_ge(w_scaled, n + 1)
                        load_weight(n, r)
                    if not last:
                        sp.wait_ge(h_psum_ready, (b + 1) * UPB * HT + ONE)
                        load_batch(b + 2, r)
                    sp.wait_ge(o_masked, (b + 1) * UPB + FREE2)
                    sp.dma_start(masked_out[ds(b, 1), :, :].rearrange("a s t -> (a s) t"), o_sb[:, r, :])\
                      .then_inc(o_stored[r], 16)

            run_steps(sp, step)

            for r in range(2):
                sp.wait_ge(o_stored[r], 16 * STEPS + DMA)

            def load_o(b, r):
                sp.dma_start(o_in[:, r, :], masked_out[ds(b, 1), :, :].rearrange("a s t -> (a s) t"))\
                  .then_inc(o_in_loaded[r], 16)

            def load_x(b, r):
                sp.dma_start(x2[:, r, :], x[ds(b, 1), :, :].rearrange("a c t -> (a c) t"))\
                  .then_inc(x2_loaded[r], 16)

            sp.wait_ge(w_scaled, NT + FREE2)
            sp.wait_ge(w_rounded, NT)
            for r in range(2):
                load_o(r, r)
                load_x(r, r)

            def step2(i, last):
                for r in range(2):
                    b = i * 2 + r
                    if not last:
                        sp.wait_ge(q_clipped, b + 1)
                        load_o(b + 2, r)
                    sp.wait_ge(y_ready, (b + 1) * NC + FREE4)
                    sp.dma_start(out[ds(b, 1), :, :].rearrange("a s n -> (a s) n"), y_sb[:, r, :])\
                      .then_inc(y_stored[r], 16)
                    if not last:
                        load_x(b + 2, r)

            with sp.Fori(0, STEPS - 1) as i:
                step2(i, False)
            step2(STEPS - 1, True)
            for r in range(2):
                sp.wait_ge(y_stored[r], 16 * STEPS + DMA)

        @block.gpsimd
        def _(pool):
            pool.iota(time[:, :], pattern=[[1, T]], base=0, channel_multiplier=0,
                      allow_small_or_imprecise_dtypes=True).then_inc(iota_ready, 1)
            pool.iota(chan[:, :], pattern=[[0, 1]], base=0, channel_multiplier=1,
                      allow_small_or_imprecise_dtypes=True).then_inc(iota_ready, 1)
            pool.memset(ident[:, :], 0.0).then_inc(ident_zeroed, 1)
            pool.wait_ge(ident_zeroed, 1)
            pool.affine_select(out=ident[:, :], in_=ident[:, :], compare_op=ALU.not_equal, fill=1.0,
                               base=0, pattern=[[-1, P]], channel_multiplier=1).then_inc(ident_ready, 1)
            pool.wait_ge(w_pmax_ready, 1)
            pool.partition_all_reduce(w_amax, w_pmax, P, bass.bass_isa.ReduceOp.max).then_inc(w_amax_ready, 1)
            v, c = wv[:, 0, :], wv[:, 1, :]

            def step(i, scan, quant, trans, last):
                if quant:
                    for r in range(2):
                        n = i * 2 + r - 2 * SCAN
                        pool.wait_ge(w_round_ready, n + 1)
                        pool.tensor_tensor(v, v, c, ALU.add).then_inc(w_added, 1)
                        pool.wait_ge(w_added, n + 1)
                        if not isinstance(n, int) or n > 0:
                            pool.wait_ge(w_transposed, n * 2)
                        pool.tensor_tensor(wq[:, :], v, c, ALU.subtract).then_inc(w_rounded, 1)

            for first, end, scan, quant, trans in SEGMENTS:
                if quant and end - first == 1:
                    step(first, scan, quant, trans, False)
                elif quant:
                    with pool.Fori(first, end) as i:
                        step(i, scan, quant, trans, False)

            pool.wait_ge(o_pmax_ready, 1)
            pool.partition_all_reduce(o_amax, o_pmax, P, bass.bass_isa.ReduceOp.max).then_inc(o_amax_ready, 1)
            pool.wait_ge(bias_loaded, 16)
            with pool.Fori(0, STEPS) as i:
                for r in range(2):
                    pool.wait_ge(x2_loaded[r], (i + 1) * 16)
                    pool.tensor_tensor(x2[:, r, :], x2[:, r, :], bias_sb[:, :], ALU.add).then_inc(xb_ready, 1)

        @block.scalar
        def _(act):
            act.sem_inc(w_scaled, FREE2)
            act.sem_inc(o_raw_ready, ONE)

            def gelu(u, b, ub):
                for t in range(HT):
                    act.wait_ge(h_psum_ready, u * HT + t + 1 + ONE)
                    act.sem_inc(gelu_turn, 1)
                    act.activation(h_sb[:, ub, t, :], ps_h[:, t, :], ACT.Gelu,
                                   bias=hbias[:, t, ds(b, 1)]).then_inc(gelu_done, 1)

            def add_b2(u, ub):
                act.wait_ge(o_psum_ready, u + 1 + ONE)
                act.wait_ge(o_masked, u + 1)
                act.activation(o_raw[:, ub, :], ps_o[:, :], ACT.Identity, bias=b2_sb[:, :])\
                   .then_inc(o_raw_ready, 1)

            act.wait_ge(params_loaded, 48)
            act.wait_ge(hbias_ready, 1)
            gelu(0, 0, 0)

            def step(i, scan, quant, trans, last):
                for r in range(2):
                    b = i * 2 + r
                    for p in range(UPB):
                        u = b * UPB + p
                        if not (last and r == 1 and p == 1):
                            act.wait_ge(o_psum_ready, u + ONE)
                            gelu(u + 1, b + (p + 1) // UPB, (p + 1) % 2)
                        add_b2(u, p)
                    if quant:
                        n = b - 2 * SCAN
                        if isinstance(i, int) and r == 0:
                            act.wait_ge(w_scale_ready, 1)
                        act.wait_ge(wt_loaded[r], (i + 1 + SCAN) * 16)
                        if not isinstance(n, int) or n > 0:
                            act.wait_ge(w_rounded, n)
                        act.activation(wv[:, 0, :], wt[:, r, :], ACT.Copy, scale=w_scale).then_inc(w_scaled, 1)

            run_steps(act, step)

            def evacuate(b, r, n):
                act.wait_ge(qT_psum, b * NC + n + 1 + ONE)
                act.activation(qT[:, r, n * GT:(n + 1) * GT, :],
                               t_banks[n].rearrange("p (k s) -> p k s", k=GT), ACT.Copy).then_inc(qT_ready, 1)

            for n in range(NC):
                evacuate(0, 0, n)

            def step2(i, last):
                for r in range(2):
                    b = i * 2 + r
                    if last and r == 1:
                        continue
                    act.wait_ge(y_psum, b * NC + ONE)
                    for n in range(NC):
                        evacuate(b + 1, 1 - r, n)

            with act.Fori(0, STEPS - 1) as i:
                step2(i, False)
            step2(STEPS - 1, True)

        @block.vector
        def _(dve):
            dve.sem_inc(o_masked, FREE2)
            dve.sem_inc(wt_scanned, FREE2)
            dve.sem_inc(y_ready, FREE4)
            dve.sem_inc(o_scanned, ONE)
            dve.sem_inc(w_stored, ONE)
            dve.wait_ge(ids_loaded, 48)
            dve.tensor_copy(ids_f[:, :], ids_i[:, :]).then_inc(const_step, 1)
            dve.tensor_copy(counts_f[:, :], counts_i[:, :]).then_inc(const_step, 1)
            dve.tensor_copy(lens_f[:, :], lens_i[:, :]).then_inc(const_step, 1)
            dve.wait_ge(iota_ready, 2)
            dve.wait_ge(const_step, 3)
            dve.tensor_scalar(onehot[:, :], ids_f[0:NSESS, :], chan[0:NSESS, :], None, ALU.is_equal)\
               .then_inc(onehot_ready, 1)
            dve.tensor_scalar(cmask[:, :], counts_f[:, :], chan[:, :], None, ALU.is_gt).then_inc(const_step, 1)
            dve.wait_ge(const_step, 4)

            def mask_weight(b, r, loads):
                dve.wait_ge(wraw_loaded[r], loads * 16)
                dve.tensor_scalar(wb[:, r, :], wraw[:, r, :], cmask[:, ds(b, 1)], None, ALU.mult)\
                   .then_inc(wb_ready, 1)

            mask_weight(0, 0, 1)
            dve.wait_ge(hbias_psum, 1)
            dve.tensor_copy(hbias[:, :, :], ps_o[:, 0:HT * B].rearrange("p (t b) -> p t b", t=HT))\
               .then_inc(hbias_ready, 1)

            def weight_scale():
                dve.wait_ge(wt_scanned, NT + FREE2)
                dve.tensor_reduce(w_pmax, w_max[:, :], AX.X, ALU.max).then_inc(w_pmax_ready, 1)
                dve.wait_ge(w_amax_ready, 1)
                dve.tensor_scalar(w_clip, w_amax, EPS, None, ALU.max).then_inc(scale_step, 1)
                dve.wait_ge(scale_step, 1)
                dve.reciprocal(w_rec, w_clip).then_inc(scale_step, 1)
                dve.wait_ge(scale_step, 2)
                dve.tensor_scalar(w_scale, w_rec, E4M3_MAX, None, ALU.mult).then_inc(w_scale_ready, 1)
                dve.wait_ge(w_scale_ready, 1)
                dve.reciprocal(w_inv, w_scale).then_inc(scale_step, 1)

            def step(i, scan, quant, trans, last):
                if quant and isinstance(i, int):
                    weight_scale()
                for r in range(2):
                    b = i * 2 + r
                    if not (last and r == 1):
                        dve.wait_ge(h_psum_ready, b * UPB * HT + ONE)
                        mask_weight(b + 1, 1 - r, i + 1 + r)
                    for p in range(UPB):
                        u = b * UPB + p
                        part = o_sb[:, r, p * UNIT:(p + 1) * UNIT]
                        dve.wait_ge(o_raw_ready, u + 1 + ONE)
                        if p == 0:
                            dve.wait_ge(o_stored[r], i * 16 + DMA)
                            dve.wait_ge(o_scanned, u + ONE)
                        dve.scalar_tensor_tensor(part, time[:, p * UNIT:(p + 1) * UNIT], lens_f[:, ds(b, 1)],
                                                 o_raw[:, p, :], ALU.is_lt, ALU.mult).then_inc(o_masked, 1)
                        dve.wait_ge(o_masked, u + 1 + FREE2)
                        dve.tensor_reduce(o_max[:, ds(u, 1)], part, AX.X, ALU.max,
                                          apply_absolute_value=True).then_inc(o_scanned, 1)
                        if scan:
                            dve.wait_ge(wt_loaded[p], (b + 1) * 16)
                            dve.tensor_reduce(w_max[:, ds(u, 1)], wt[:, p, :], AX.X, ALU.max,
                                              apply_absolute_value=True).then_inc(wt_scanned, 1)
                        if trans:
                            n = b - 2 * SCAN - 2
                            dve.wait_ge(w_transposed, n * 2 + p + 1)
                            dve.tensor_scalar(wqT[:, p * KT // 2:(p + 1) * KT // 2, ds(n * P, P)],
                                              ps_t[:, p, :].rearrange("k (t n) -> k t n", n=P),
                                              E4M3_MAX, -E4M3_MAX, ALU.min, ALU.max).then_inc(w_stored, 1)
                    if quant:
                        n = b - 2 * SCAN
                        dve.wait_ge(w_scaled, n + 1 + FREE2)
                        dve.tensor_scalar(wv[:, 1, :].bitcast(i32), wv[:, 0, :].bitcast(i32), EXPONENT, None,
                                          ALU.bitwise_and).then_inc(w_exponent, 1)
                        dve.wait_ge(w_exponent, n + 1)
                        dve.tensor_scalar(wv[:, 1, :], wv[:, 1, :], E4M3_MIN_NORMAL, ROUND_AT,
                                          ALU.max, ALU.mult).then_inc(w_round_ready, 1)

            run_steps(dve, step)

            dve.wait_ge(o_scanned, B * UPB + ONE)
            dve.tensor_reduce(o_pmax, o_max[:, :], AX.X, ALU.max).then_inc(o_pmax_ready, 1)
            dve.wait_ge(o_amax_ready, 1)
            dve.tensor_scalar(o_pmax, o_amax, EPS, None, ALU.max).then_inc(scale_step, 1)
            dve.wait_ge(scale_step, 4)
            dve.reciprocal(o_rec, o_pmax).then_inc(scale_step, 1)
            dve.wait_ge(scale_step, 5)
            dve.tensor_scalar(o_scale, o_rec, E5M2_MAX, None, ALU.mult).then_inc(scale_step, 1)
            dve.wait_ge(scale_step, 6)
            dve.reciprocal(o_inv, o_scale).then_inc(scale_step, 1)
            dve.wait_ge(scale_step, 7)
            dve.tensor_tensor(y_scale, o_inv, w_inv, ALU.mult).then_inc(scale_step, 1)
            dve.wait_ge(scale_step, 8)

            def quantize(b, r, loads):
                dve.wait_ge(o_in_loaded[r], loads * 16)
                if not isinstance(b, int) or b > 0:
                    dve.wait_ge(q_ready, b)
                dve.tensor_scalar(v_sb, o_in[:, r, :], o_scale, E5M2_MAX, ALU.mult, ALU.min)\
                   .then_inc(q_clipped, 1)
                dve.wait_ge(q_clipped, b + 1)
                dve.sem_inc(q_turn, 1)
                dve.tensor_scalar(q8[:, r, :], v_sb, -E5M2_MAX, None, ALU.max, saturate=False)\
                   .then_inc(q_ready, 1)

            quantize(0, 0, 1)

            def step2(i, last):
                for r in range(2):
                    b = i * 2 + r
                    if not (last and r == 1):
                        dve.wait_ge(qT_psum, b * NC + ONE)
                        quantize(b + 1, 1 - r, i + 1 + r)
                    dve.wait_ge(xb_ready, b + 1)
                    dve.wait_ge(y_stored[r], i * 16 + DMA)
                    for n in range(NC):
                        cols = slice(n * BANK, (n + 1) * BANK)
                        dve.wait_ge(y_psum, b * NC + n + 1 + ONE)
                        dve.scalar_tensor_tensor(y_sb[:, r, cols], ps_y[n], y_scale, x2[:, r, cols],
                                                 ALU.mult, ALU.add).then_inc(y_ready, 1)

            for r in range(2):
                dve.wait_ge(o_stored[r], 16 * STEPS + DMA)
            with dve.Fori(0, STEPS - 1) as i:
                step2(i, False)
            step2(STEPS - 1, True)

        @block.tensor
        def _(pe):
            for count in (h_psum_ready, o_psum_ready, qT_psum, y_psum):
                pe.sem_inc(count, ONE)
            pe.wait_ge(params_loaded, 48)
            pe.wait_ge(onehot_ready, 1)
            for t in range(HT):
                last_mm = nc.tensor.matmul(ps_o[:, t * B:(t + 1) * B], bs_sb[:, t * P:(t + 1) * P],
                                           onehot[:, :], start=True, stop=True)
            last_mm.then_inc(hbias_psum, 1)

            def hidden(u, b, r, p, loads):
                if p == 0:
                    pe.wait_ge(x_loaded[r], loads * 16)
                    pe.wait_ge(wb_ready, b + 1)
                for t in range(HT):
                    if not isinstance(u, int) or u > 0:
                        pe.wait_ge(gelu_done, (u - 1) * HT + t + 1)
                    for c in range(2):
                        at = p * UNIT + c * BANK
                        mm = nc.tensor.matmul(ps_h[:, t, c * BANK:(c + 1) * BANK], wb[:, r, t * P:(t + 1) * P],
                                              x_sb[:, r, at:at + BANK], start=True, stop=True)
                    mm.then_inc(h_psum_ready, 1)

            def project(u, p):
                pe.wait_ge(gelu_done, (u + 1) * HT)
                pe.wait_ge(o_raw_ready, u + ONE)
                for c in range(2):
                    for t in range(HT):
                        mm = nc.tensor.matmul(ps_o[:, c * BANK:(c + 1) * BANK], w2_sb[:, t, :],
                                              h_sb[:, p, t, c * BANK:(c + 1) * BANK],
                                              start=(t == 0), stop=(t == HT - 1))
                mm.then_inc(o_psum_ready, 1)

            hidden(0, 0, 0, 0, 1)
            pe.wait_ge(hbias_ready, 1)
            pe.wait_ge(ident_ready, 1)

            def step(i, scan, quant, trans, last):
                for r in range(2):
                    b = i * 2 + r
                    for p in range(UPB):
                        u = b * UPB + p
                        if p == 0:
                            hidden(u + 1, b, r, 1, i + 1)
                            pe.sem_inc(x_free, 0) if False else None
                        elif not (last and r == 1):
                            hidden(u + 1, b + 1, 1 - r, 0, i + 1 + r)
                        project(u, p)
                        if trans:
                            n = b - 2 * SCAN - 2
                            pe.wait_ge(w_rounded, n + 1)
                            pe.wait_ge(w_stored, n * 2 + ONE)
                            for k in range(KT // 2):
                                kt = p * KT // 2 + k
                                mm = nc.tensor.transpose(ps_t[:, p, k * P:(k + 1) * P],
                                                         wq[:, kt * P:(kt + 1) * P], ident[:, :])
                            mm.then_inc(w_transposed, 1)

            run_steps(pe, step)

            def transpose(b, r, n):
                pe.wait_ge(q_ready, b + 1)
                if not isinstance(b, int) or b > 0:
                    pe.wait_ge(qT_ready, b * NC)
                pe.sem_inc(transpose_turn, 1)
                for k in range(GT):
                    kt = n * GT + k
                    mm = nc.tensor.matmul(t_banks[n][:, k * P:(k + 1) * P], q8[:, r, kt * P:(kt + 1) * P],
                                          ident[:, :], start=True, stop=True)
                mm.then_inc(qT_psum, 1)

            pe.wait_ge(o_raw_ready, B * UPB + ONE)
            pe.wait_ge(w_stored, NT * 2 + ONE)
            for n in range(NC):
                transpose(0, 0, n)

            def step2(i, last):
                for r in range(2):
                    b = i * 2 + r
                    pe.wait_ge(qT_ready, (b + 1) * NC)
                    for n in range(NC):
                        pe.wait_ge(y_ready, b * NC + n + 1)
                        for k in range(KT):
                            mm = nc.tensor.matmul(ps_y[n], qT[:, r, k, :], wqT[:, k, n * BANK:(n + 1) * BANK],
                                                  start=(k == 0), stop=(k == KT - 1))
                        mm.then_inc(y_psum, 1)
                        if not (last and r == 1):
                            transpose(b + 1, 1 - r, n)

            with pe.Fori(0, STEPS - 1) as i:
                step2(i, False)
            step2(STEPS - 1, True)


_INS = ["x", "itok_B_0_7", "itok_B_2182_4065", "_lenS", "L0_cond_W_sess", "L0_cond_b_sess", "L0_cond_W2",
        "L0_cond_b2", "L0_ffn_weight", "L0_ffn_bias"]


def kernel(**inputs):
    import concourse.bacc as bacc
    from concourse.bass_utils import run_bass_kernel_spmd

    nc = bacc.Bacc("TRN2", target_bir_lowering=False, num_devices=1)
    arrays, args = {}, []
    for name in _INS:
        a = np.ascontiguousarray(inputs[name])
        arrays[f"in_{name}"] = a
        args.append(nc.dram_tensor(f"in_{name}", a.shape, mybir.dt.from_np(a.dtype), kind="ExternalInput").ap())
    shape = inputs["x"].shape
    out = nc.dram_tensor("out", shape, mybir.dt.float32, kind="ExternalOutput").ap()
    masked_out = nc.dram_tensor("masked_out", shape, mybir.dt.float32, kind="Internal").ap()
    adaln_ffn(nc, *args, out, masked_out)
    return run_bass_kernel_spmd(nc, [arrays], core_ids=[0]).results[0]["out"]
```

```python
import concourse.bass as bass
from concourse import mybir
from contextlib import ExitStack
import numpy as np


def adaln_ffn(nc, x, ids, lens, counts, w_sess, b_sess, w2, b2, weight, bias, out, masked_out):
    fp32, bf16, fp8, i32 = mybir.dt.float32, mybir.dt.bfloat16, mybir.dt.float8e5, mybir.dt.int32
    fp32r = mybir.dt.float32r
    ALU, ACT, AX = mybir.AluOpType, mybir.ActivationFunctionType, mybir.AxisListType
    ds = bass.ds

    P = 128
    B, C, T = x.shape
    NSESS, _, HID = w_sess.shape
    HT = HID // P
    F = weight.shape[0]
    BANK = 512
    UNIT = 2 * BANK
    UPB = T // UNIT
    NT = F // P
    KT = T // P
    NC = F // BANK
    STEPS = B // 2
    E4M3_MAX, E5M2_MAX, EPS = 448.0, 57344.0, 1e-12
    EXPONENT = 0x7F800000
    E4M3_MIN_NORMAL = 2.0 ** -6
    ROUND_AT = 1.5 * 2.0 ** 20
    assert C == P and UPB == 2 and NT == KT and B == 2 * NT

    SCAN = NT // 4
    QUANT = SCAN + NT // 2
    SEGMENTS = [(0, SCAN, True, False, False), (SCAN, SCAN + 1, False, True, False),
                (SCAN + 1, QUANT, False, True, True), (QUANT, QUANT + 1, False, False, True),
                (QUANT + 1, STEPS - 1, False, False, False), (STEPS - 1, STEPS, False, False, False)]
    CUTS = 2
    CUT = [slice(k * T // CUTS, (k + 1) * T // CUTS) for k in range(CUTS)]
    ALL = slice(0, T)
    FREE2, FREE4 = 2, 4
    ONE, DMA = 1, 16

    with ExitStack() as ctx:
        def sb(name, shape, dt):
            return ctx.enter_context(nc.sbuf_tensor(name, shape, dt))

        def sem(name):
            return ctx.enter_context(nc.semaphore(name))

        ids_i = sb("ids_i", [P, B], i32)
        counts_i = sb("counts_i", [P, B], i32)
        lens_i = sb("lens_i", [P, B], i32)
        ids_f = sb("ids_f", [P, B], fp32)
        counts_f = sb("counts_f", [P, B], fp32)
        lens_f = sb("lens_f", [P, UPB, B], fp32)
        chan = sb("chan", [P, 1], fp32)
        time = sb("time", [P, UNIT], fp32)
        onehot = sb("onehot", [NSESS, B], fp32)
        cmask = sb("cmask", [P, B], fp32)
        bs_sb = sb("bs_sb", [NSESS, HID], fp32)
        hbias = sb("hbias", [P, HT, B], fp32)
        w2_sb = sb("w2_sb", [P, HT, P], fp32)
        b2_sb = sb("b2_sb", [P, 1], fp32)
        wqT = sb("wqT", [P, KT, F], bf16)
        w_max = sb("w_max", [P, NT], fp32)
        o_max = sb("o_max", [P, B * UPB], fp32)
        scales = sb("scales", [P, 13], fp32)
        w_pmax, w_amax, w_clip, w_rec, w_scale, w_inv = (scales[:, k:k + 1] for k in range(6))
        o_pmax, o_amax, o_clip, o_rec, o_scale, o_inv, y_scale = (scales[:, k:k + 1] for k in range(6, 13))

        x_sb = sb("x_sb", [P, 2, T], fp32)
        wraw = sb("wraw", [P, 2, HID], fp32)
        wh = sb("wh", [P, 2, HID], fp32r)
        wl = sb("wl", [P, 2, HID], fp32r)
        xh = sb("xh", [P, 2, UNIT], fp32r)
        xl = sb("xl", [P, 2, UNIT], fp32r)
        h_sb = sb("h_sb", [P, 2, HT, UNIT], fp32)
        o_raw = sb("o_raw", [P, 2, UNIT], fp32)
        o_sb = sb("o_sb", [P, 2, T], fp32)
        wt = sb("wt", [P, 2, T], fp32)
        ws = sb("ws", [P, 2, T], fp32)
        wp = sb("wp", [P, 2, T], fp32)
        wq = sb("wq", [P, 2, T], bf16)
        qT = ws[:, 0, :].bitcast(bf16).rearrange("p (r k t) -> p r k t", r=2, k=KT)
        bias_sb = h_sb[:, 1, :, :].rearrange("p a n -> p (a n)")
        qb = x_sb[:, 0, :].bitcast(bf16).rearrange("p (r t) -> p r t", r=2)
        q8 = x_sb[:, 1, 0:T // 2].bitcast(fp8).rearrange("p (r t) -> p r t", r=2)
        o_in, x2, y_sb = wt, wp, o_sb
        scan_sb = (wt, ws)

        ps_h = ctx.enter_context(nc.psum_tensor("ps_h", [P, HT, UNIT], fp32))
        ps_o = ctx.enter_context(nc.psum_tensor("ps_o", [P, UNIT], fp32))
        ps_y = [ps_h[:, n // 2, n % 2 * BANK:(n % 2 + 1) * BANK] for n in range(NC)]

        params_loaded = sem("params_loaded")
        ids_loaded = sem("ids_loaded")
        bias_loaded = sem("bias_loaded")
        iota_ready = sem("iota_ready")
        const_step = sem("const_step")
        onehot_ready = sem("onehot_ready")
        hbias_psum = sem("hbias_psum")
        hbias_ready = sem("hbias_ready")
        x_loaded = [sem(f"x_loaded{r}") for r in range(2)]
        x_first = [sem(f"x_first{p}") for p in range(UPB)]
        wraw_loaded = [sem(f"wraw_loaded{r}") for r in range(2)]
        wh_ready = sem("wh_ready")
        wl_ready = sem("wl_ready")
        xh_ready = sem("xh_ready")
        xl_ready = sem("xl_ready")
        h_psum_ready = sem("h_psum_ready")
        gelu_done = sem("gelu_done")
        o_psum_ready = sem("o_psum_ready")
        o_raw_ready = sem("o_raw_ready")
        o_masked = sem("o_masked")
        o_scanned = sem("o_scanned")
        o_stored = [sem(f"o_stored{r}") for r in range(2)]
        scan_loaded = [[sem(f"scan_loaded{r}{k}") for k in range(2)] for r in range(2)]
        wt_loaded = [sem(f"wt_loaded{r}") for r in range(2)]
        wt_scanned = sem("wt_scanned")
        scale_step = sem("scale_step")
        w_pmax_ready = sem("w_pmax_ready")
        w_amax_ready = sem("w_amax_ready")
        w_scale_ready = sem("w_scale_ready")
        w_scaled = sem("w_scaled")
        w_exponent = sem("w_exponent")
        w_round_ready = sem("w_round_ready")
        w_added = sem("w_added")
        w_rounded = sem("w_rounded")
        w_transposed = [sem(f"w_transposed{r}") for r in range(2)]
        o_pmax_ready = sem("o_pmax_ready")
        o_amax_ready = sem("o_amax_ready")
        o_in_loaded = [sem(f"o_in_loaded{r}") for r in range(2)]
        x2_loaded = [sem(f"x2_loaded{r}") for r in range(2)]
        qb_ready = sem("qb_ready")
        qT_cut = [sem(f"qT_cut{k}") for k in range(CUTS)]
        qT_loaded = [sem(f"qT_loaded{r}") for r in range(2)]
        xb_ready = sem("xb_ready")
        q_ready = sem("q_ready")
        y_psum = sem("y_psum")
        y_ready = sem("y_ready")
        y_stored = [sem(f"y_stored{r}") for r in range(2)]

        gelu_turn = sem("gelu_turn")
        q_turn = sem("q_turn")
        widen_turn = sem("widen_turn")
        load_turn = sem("load_turn")
        transpose_turn = sem("transpose_turn")

        block = ctx.enter_context(nc.Block())

        def run_steps(eng, step):
            for first, end, scan, scale, trans in SEGMENTS:
                if end - first == 1:
                    step(first, scan, scale, trans, end == STEPS)
                else:
                    with eng.Fori(first, end) as i:
                        step(i, scan, scale, trans, False)

        @block.sync
        def _(sp):
            for r in range(2):
                for count in (o_stored[r], y_stored[r], w_transposed[r], qT_loaded[r]):
                    sp.sem_inc(count, DMA)

            def load_x(b, r):
                sp.dma_start(x_sb[:, r, :], x[ds(b, 1), :, :].rearrange("a c t -> (a c) t"))\
                  .then_inc(x_loaded[r], 16)

            def load_session_weight(b, r):
                sid = sp.value_load(ids_i[0:1, ds(b, 1)], min_val=0, max_val=NSESS - 1)
                sp.dma_start(wraw[:, r, :], w_sess[ds(sid, 1), :, :].rearrange("a c h -> (a c) h"))\
                  .then_inc(wraw_loaded[r], 16)

            def load_weight(tile, buffer, loaded):
                sp.dma_start(buffer, weight[ds(tile * P, P), :]).then_inc(loaded, 16)

            for dst, src in ((ids_i, ids), (counts_i, counts), (lens_i, lens)):
                sp.dma_start(dst[:, :], src.partition_broadcast(P)).then_inc(ids_loaded, 16)
            for p in range(UPB):
                cols = slice(p * UNIT, (p + 1) * UNIT)
                sp.dma_start(x_sb[:, 0, cols], x[0, :, cols]).then_inc(x_first[p], 16)
            sp.dma_start(bs_sb[:, :], b_sess).then_inc(params_loaded, 16)
            sp.dma_start(w2_sb[:, :, :], w2.rearrange("(j p) s -> p j s", p=P)).then_inc(params_loaded, 16)
            sp.dma_start(b2_sb[:, :], b2.rearrange("(p a) -> p a", a=1)).then_inc(params_loaded, 16)
            sp.wait_ge(ids_loaded, 48)
            load_session_weight(0, 0)
            load_session_weight(1, 1)
            load_x(1, 1)

            def load_o(b, r):
                sp.dma_start(o_in[:, r, :], masked_out[ds(b, 1), :, :].rearrange("a s t -> (a s) t"))\
                  .then_inc(o_in_loaded[r], 16)

            def load_x_again(b, r):
                sp.dma_start(x2[:, r, :], x[ds(b, 1), :, :].rearrange("a c t -> (a c) t"))\
                  .then_inc(x2_loaded[r], 16)

            def store_o(b, r):
                sp.dma_start(masked_out[ds(b, 1), :, :].rearrange("a s t -> (a s) t"), o_sb[:, r, :])\
                  .then_inc(o_stored[r], 16)

            def step(i, scan, scale, trans, last):
                if last:
                    sp.wait_ge(w_rounded, NT + ONE)
                    for r in range(2):
                        load_o(r, r)
                        load_x_again(r, r)
                for r in range(2):
                    b = i * 2 + r
                    if not last:
                        sp.wait_ge(xl_ready, (b + 1) * UPB)
                        load_x(b + 2, r)
                        sp.wait_ge(wl_ready, b + 1)
                        sp.sem_inc(load_turn, 1)
                        load_session_weight(b + 2, r)
                    if scan:
                        for k in range(2):
                            sp.wait_ge(wt_scanned, b * 2 + k + 1)
                            load_weight(b * 2 + k, scan_sb[r][:, k, :], scan_loaded[r][k])
                    if scale:
                        n = b - 2 * SCAN
                        sp.wait_ge(wt_scanned, NT + FREE4)
                        if not isinstance(n, int):
                            sp.wait_ge(w_scaled, (n - 1) * UPB)
                        load_weight(n, wt[:, r, :], wt_loaded[r])
                    if trans:
                        n = b - 2 * SCAN - 2
                        sp.wait_ge(w_rounded, n + 1 + ONE)
                        sp.sem_inc(transpose_turn, 1)
                        sp.dma_start_transpose(wqT[:, :, ds(n * P, P)], wq[:, r, :]).then_inc(w_transposed[r], 16)
                    sp.wait_ge(o_masked, (b + 1) * UPB + FREE2)
                    if not (last and r == 1):
                        store_o(b, r)

            run_steps(sp, step)

            def transpose(r, cols, done, landed):
                sp.wait_ge(qb_ready, done + 1 + ONE)
                sp.sem_inc(transpose_turn, 1)
                sp.dma_start_transpose(qT[:, r, cols.start // P:cols.stop // P, :], qb[:, r, cols])\
                  .then_inc(landed, 16)

            for k in range(CUTS):
                transpose(0, CUT[k], k, qT_cut[k])
            sp.dma_start(bias_sb, bias.partition_broadcast(P)).then_inc(bias_loaded, 16)
            store_o(B - 1, 1)
            for r in range(2):
                sp.wait_ge(o_stored[r], 16 * STEPS + DMA)

            def step2(i, last):
                for r in range(2):
                    b = i * 2 + r
                    if not last:
                        sp.wait_ge(q_ready, b + CUTS)
                        load_o(b + 2, r)
                    if not (last and r == 1):
                        sp.wait_ge(y_psum, b * NC + ONE)
                        sp.sem_inc(load_turn, 1)
                        transpose(1 - r, ALL, b + CUTS, qT_loaded[1 - r])
                    sp.wait_ge(y_ready, (b + 1) * NC + FREE4)
                    sp.dma_start(out[ds(b, 1), :, :].rearrange("a s n -> (a s) n"), y_sb[:, r, :])\
                      .then_inc(y_stored[r], 16)
                    if not last:
                        load_x_again(b + 2, r)

            with sp.Fori(0, STEPS - 1) as i:
                step2(i, False)
            step2(STEPS - 1, True)
            for r in range(2):
                sp.wait_ge(y_stored[r], 16 * STEPS + DMA)

        @block.gpsimd
        def _(pool):
            pool.sem_inc(w_rounded, ONE)
            pool.iota(time[:, :], pattern=[[1, UNIT]], base=0, channel_multiplier=0,
                      allow_small_or_imprecise_dtypes=True).then_inc(iota_ready, 1)
            pool.iota(chan[:, :], pattern=[[0, 1]], base=0, channel_multiplier=1,
                      allow_small_or_imprecise_dtypes=True).then_inc(iota_ready, 1)

            def split_x_rest(u, r, p):
                pool.wait_ge(xh_ready, u + 1)
                pool.tensor_tensor(xl[:, p, :], x_sb[:, r, p * UNIT:(p + 1) * UNIT], xh[:, p, :].bitcast(fp32),
                                   ALU.subtract).then_inc(xl_ready, 1)

            def step(i, scan, scale, trans, last):
                for r in range(2):
                    b = i * 2 + r
                    n = b - 2 * SCAN - 2
                    v, c = ws[:, r, :], wp[:, r, :]
                    for p in range(UPB):
                        if scan:
                            split_x_rest((b + 1) * UPB + p, 1 - r, p)
                        if trans and p == 0:
                            pool.wait_ge(w_round_ready, n + 1)
                            pool.tensor_tensor(v, v, c, ALU.add).then_inc(w_added, 1)
                        if trans and p == 1:
                            pool.wait_ge(w_added, n + 1)
                            pool.wait_ge(w_transposed[r], (i - SCAN - 1) * 16 + DMA)
                            pool.tensor_tensor(wq[:, r, :], v, c, ALU.subtract).then_inc(w_rounded, 1)

            for first, end, scan, scale, trans in SEGMENTS:
                if scale and end - first == 1:
                    pool.wait_ge(w_pmax_ready, 1)
                    pool.partition_all_reduce(w_amax, w_pmax, P, bass.bass_isa.ReduceOp.max)\
                        .then_inc(w_amax_ready, 1)
                if end - first == 1:
                    step(first, scan, scale, trans, end == STEPS)
                else:
                    with pool.Fori(first, end) as i:
                        step(i, scan, scale, trans, False)

            pool.wait_ge(o_pmax_ready, 1)
            pool.partition_all_reduce(o_amax, o_pmax, P, bass.bass_isa.ReduceOp.max).then_inc(o_amax_ready, 1)
            pool.wait_ge(bias_loaded, 16)
            with pool.Fori(0, STEPS) as i:
                for r in range(2):
                    pool.wait_ge(x2_loaded[r], (i + 1) * 16)
                    pool.tensor_tensor(x2[:, r, :], x2[:, r, :], bias_sb[:, :], ALU.add).then_inc(xb_ready, 1)

        @block.scalar
        def _(act):
            act.sem_inc(qb_ready, ONE)
            act.sem_inc(o_raw_ready, ONE)

            def gelu(u, b, ub):
                for t in range(HT):
                    act.wait_ge(h_psum_ready, u * HT + t + 1 + ONE)
                    act.sem_inc(gelu_turn, 1)
                    act.activation(h_sb[:, ub, t, :], ps_h[:, t, :], ACT.Gelu,
                                   bias=hbias[:, t, ds(b, 1)]).then_inc(gelu_done, 1)

            def add_b2(u, ub):
                act.wait_ge(o_psum_ready, u + 1 + ONE)
                act.wait_ge(o_masked, u + 1)
                act.activation(o_raw[:, ub, :], ps_o[:, :], ACT.Identity, bias=b2_sb[:, :])\
                   .then_inc(o_raw_ready, 1)

            def split_x(u, r, p, loads):
                act.wait_ge(x_loaded[r], loads * 16)
                if not isinstance(u, int) or u > 1:
                    act.wait_ge(h_psum_ready, (u - 1) * HT + ONE)
                act.activation(xh[:, p, :], x_sb[:, r, p * UNIT:(p + 1) * UNIT], ACT.Copy).then_inc(xh_ready, 1)

            act.wait_ge(params_loaded, 48)
            act.wait_ge(hbias_ready, 1)
            gelu(0, 0, 0)

            def step(i, scan, scale, trans, last):
                for r in range(2):
                    b = i * 2 + r
                    for p in range(UPB):
                        u = b * UPB + p
                        if not (last and r == 1):
                            split_x((b + 1) * UPB + p, 1 - r, p, i + 1)
                        if not (last and r == 1 and p == 1):
                            act.wait_ge(o_psum_ready, u + ONE)
                            gelu(u + 1, b + (p + 1) // UPB, (p + 1) % 2)
                        n, cols = b - 2 * SCAN - 1, slice(p * UNIT, (p + 1) * UNIT)
                        if (scale or trans) and (not isinstance(n, int) or 0 <= n < NT):
                            if isinstance(n, int) and n == 0:
                                act.wait_ge(w_scale_ready, 1)
                            else:
                                act.wait_ge(w_rounded, n - 1 + ONE)
                            act.wait_ge(wt_loaded[1 - r], (i + r - SCAN) * 16)
                            act.activation(ws[:, 1 - r, cols], wt[:, 1 - r, cols], ACT.Copy, scale=w_scale)\
                               .then_inc(w_scaled, 1)
                        add_b2(u, p)

            run_steps(act, step)

            def widen(b, r, cols, done, uses):
                act.wait_ge(q_ready, done + 1)
                act.wait_ge(qT_loaded[r], uses * 16 + DMA)
                act.sem_inc(widen_turn, 1)
                act.activation(qb[:, r, cols], q8[:, r, cols], ACT.Copy).then_inc(qb_ready, 1)

            for k in range(CUTS):
                widen(0, 0, CUT[k], k, 0)
            widen(1, 1, ALL, CUTS, 0)
            for k in range(CUTS):
                act.wait_ge(qT_cut[k], 16)
            with act.Fori(0, STEPS - 1) as i:
                widen(i * 2 + 2, 0, ALL, i * 2 + 1 + CUTS, i)
                widen(i * 2 + 3, 1, ALL, i * 2 + 2 + CUTS, i + 1)

        @block.vector
        def _(dve):
            dve.sem_inc(o_masked, FREE2)
            dve.sem_inc(wt_scanned, FREE4)
            dve.sem_inc(y_ready, FREE4)
            dve.sem_inc(o_scanned, ONE)
            dve.wait_ge(ids_loaded, 48)
            dve.tensor_copy(ids_f[:, :], ids_i[:, :]).then_inc(const_step, 1)
            dve.tensor_copy(counts_f[:, :], counts_i[:, :]).then_inc(const_step, 1)
            for p in range(UPB):
                dve.tensor_scalar(lens_f[:, p, :], lens_i[:, :], float(-p * UNIT), None, ALU.add)\
                   .then_inc(const_step, 1)
            dve.wait_ge(iota_ready, 2)
            dve.wait_ge(const_step, 4)
            dve.tensor_scalar(onehot[:, :], ids_f[0:NSESS, :], chan[0:NSESS, :], None, ALU.is_equal)\
               .then_inc(onehot_ready, 1)
            dve.tensor_scalar(cmask[:, :], counts_f[:, :], chan[:, :], None, ALU.is_gt).then_inc(const_step, 1)
            dve.wait_ge(const_step, 5)

            def mask_weight(b, r, loads):
                dve.wait_ge(wraw_loaded[r], loads * 16)
                mask = cmask[:, ds(b, 1)]
                dve.tensor_scalar(wh[:, r, :], wraw[:, r, :], mask, None, ALU.mult).then_inc(wh_ready, 1)
                dve.wait_ge(wh_ready, b + 1)
                dve.scalar_tensor_tensor(wl[:, r, :], wraw[:, r, :], mask, wh[:, r, :].bitcast(fp32),
                                         ALU.mult, ALU.subtract).then_inc(wl_ready, 1)

            def split_x_rest(u, r, p):
                dve.wait_ge(xh_ready, u + 1)
                if not isinstance(u, int) or u > 0:
                    dve.wait_ge(xl_ready, u)
                dve.tensor_tensor(xl[:, p, :], x_sb[:, r, p * UNIT:(p + 1) * UNIT], xh[:, p, :].bitcast(fp32),
                                  ALU.subtract).then_inc(xl_ready, 1)

            mask_weight(0, 0, 1)
            for p in range(UPB):
                dve.wait_ge(x_first[p], 16)
                dve.tensor_copy(xh[:, p, :], x_sb[:, 0, p * UNIT:(p + 1) * UNIT]).then_inc(xh_ready, 1)
                split_x_rest(p, 0, p)
            dve.wait_ge(hbias_psum, 1)
            dve.tensor_copy(hbias[:, :, :], ps_o[:, 0:HT * B].rearrange("p (t b) -> p t b", t=HT))\
               .then_inc(hbias_ready, 1)

            def weight_maximum():
                dve.wait_ge(wt_scanned, NT + FREE4)
                dve.tensor_reduce(w_pmax, w_max[:, :], AX.X, ALU.max).then_inc(w_pmax_ready, 1)

            def weight_scale():
                dve.wait_ge(w_amax_ready, 1)
                dve.tensor_scalar(w_clip, w_amax, EPS, None, ALU.max).then_inc(scale_step, 1)
                dve.wait_ge(scale_step, 1)
                dve.reciprocal(w_rec, w_clip).then_inc(scale_step, 1)
                dve.wait_ge(scale_step, 2)
                dve.tensor_scalar(w_scale, w_rec, E4M3_MAX, None, ALU.mult).then_inc(w_scale_ready, 1)
                dve.wait_ge(w_scale_ready, 1)
                dve.reciprocal(w_inv, w_scale).then_inc(scale_step, 1)

            def step(i, scan, scale, trans, last):
                for r in range(2):
                    b = i * 2 + r
                    for p in range(UPB):
                        u = b * UPB + p
                        if not scan and not (last and r == 1):
                            split_x_rest(u + 2, 1 - r, p)
                        if scale and isinstance(i, int) and r == 0:
                            if p == 0:
                                weight_maximum()
                            else:
                                weight_scale()
                        if p == 0 and not (last and r == 1):
                            dve.wait_ge(h_psum_ready, b * UPB * HT + ONE)
                            mask_weight(b + 1, 1 - r, i + 1 + r)
                        n = b - 2 * SCAN - 1
                        if (scale or trans) and (not isinstance(n, int) or 0 <= n < NT) and p == 1:
                            v, c = ws[:, 1 - r, :], wp[:, 1 - r, :]
                            dve.wait_ge(w_scaled, (n + 1) * UPB)
                            dve.tensor_scalar(c.bitcast(i32), v.bitcast(i32), EXPONENT, None,
                                              ALU.bitwise_and).then_inc(w_exponent, 1)
                            dve.wait_ge(w_exponent, n + 1)
                            dve.tensor_scalar(c, c, E4M3_MIN_NORMAL, ROUND_AT, ALU.max, ALU.mult)\
                               .then_inc(w_round_ready, 1)
                        part = o_sb[:, r, p * UNIT:(p + 1) * UNIT]
                        dve.wait_ge(o_raw_ready, u + 1 + ONE)
                        if p == 0:
                            dve.wait_ge(o_stored[r], i * 16 + DMA)
                            dve.wait_ge(o_scanned, u + ONE)
                        dve.scalar_tensor_tensor(part, time[:, :], lens_f[:, p, ds(b, 1)],
                                                 o_raw[:, p, :], ALU.is_lt, ALU.mult).then_inc(o_masked, 1)
                        dve.wait_ge(o_masked, u + 1 + FREE2)
                        dve.tensor_reduce(o_max[:, ds(u, 1)], part, AX.X, ALU.max,
                                          apply_absolute_value=True).then_inc(o_scanned, 1)
                        if scan:
                            dve.wait_ge(scan_loaded[r][p], (i + 1) * 16)
                            dve.tensor_reduce(w_max[:, ds(u, 1)], scan_sb[r][:, p, :], AX.X, ALU.max,
                                              apply_absolute_value=True).then_inc(wt_scanned, 1)
            run_steps(dve, step)

            dve.wait_ge(o_scanned, B * UPB + ONE)
            dve.tensor_reduce(o_pmax, o_max[:, :], AX.X, ALU.max).then_inc(o_pmax_ready, 1)
            dve.wait_ge(o_amax_ready, 1)
            dve.tensor_scalar(o_clip, o_amax, EPS, None, ALU.max).then_inc(scale_step, 1)
            dve.wait_ge(scale_step, 4)
            dve.reciprocal(o_rec, o_clip).then_inc(scale_step, 1)
            dve.wait_ge(scale_step, 5)
            dve.tensor_scalar(o_scale, o_rec, E5M2_MAX, None, ALU.mult).then_inc(scale_step, 1)
            dve.wait_ge(scale_step, 6)

            def quantize(r, loads, first, cols):
                if first:
                    dve.wait_ge(o_in_loaded[r], loads * 16)
                dve.sem_inc(q_turn, 1)
                dve.tensor_scalar(q8[:, r, cols], o_in[:, r, cols], o_scale, None, ALU.mult, saturate=False)\
                   .then_inc(q_ready, 1)

            for k in range(CUTS):
                quantize(0, 1, k == 0, CUT[k])
            dve.reciprocal(o_inv, o_scale).then_inc(scale_step, 1)
            dve.wait_ge(scale_step, 7)
            dve.tensor_tensor(y_scale, o_inv, w_inv, ALU.mult).then_inc(scale_step, 1)
            dve.wait_ge(scale_step, 8)

            def step2(i, last):
                for r in range(2):
                    b = i * 2 + r
                    if not (last and r == 1):
                        dve.wait_ge(qb_ready, b + CUTS - 1 + ONE)
                        quantize(1 - r, i + 1 + r, True, ALL)
                    dve.wait_ge(xb_ready, b + 1)
                    dve.wait_ge(y_stored[r], i * 16 + DMA)
                    for n in range(NC):
                        cols = slice(n * BANK, (n + 1) * BANK)
                        dve.wait_ge(y_psum, b * NC + n + 1 + ONE)
                        dve.scalar_tensor_tensor(y_sb[:, r, cols], ps_y[n], y_scale, x2[:, r, cols],
                                                 ALU.mult, ALU.add).then_inc(y_ready, 1)

            for r in range(2):
                dve.wait_ge(o_stored[r], 16 * STEPS + DMA)
            with dve.Fori(0, STEPS - 1) as i:
                step2(i, False)
            step2(STEPS - 1, True)

        @block.tensor
        def _(pe):
            for count in (h_psum_ready, o_psum_ready, y_psum):
                pe.sem_inc(count, ONE)
            pe.wait_ge(params_loaded, 48)
            pe.wait_ge(onehot_ready, 1)
            for t in range(HT):
                last_mm = nc.tensor.matmul(ps_o[:, t * B:(t + 1) * B], bs_sb[:, t * P:(t + 1) * P],
                                           onehot[:, :], start=True, stop=True)
            last_mm.then_inc(hbias_psum, 1)

            def hidden(u, b, r, p):
                if p == 0:
                    pe.wait_ge(wl_ready, b + 1)
                pe.wait_ge(xl_ready, u + 1)
                for t in range(HT):
                    if not isinstance(u, int) or u > 0:
                        pe.wait_ge(gelu_done, (u - 1) * HT + t + 1)
                    rows = slice(t * P, (t + 1) * P)
                    for c in range(2):
                        cols = slice(c * BANK, (c + 1) * BANK)
                        for k, (w, xs) in enumerate(((wl, xh), (wh, xl), (wh, xh))):
                            mm = nc.tensor.matmul(ps_h[:, t, cols], w[:, r, rows], xs[:, p, cols],
                                                  start=(k == 0), stop=(k == 2))
                    mm.then_inc(h_psum_ready, 1)

            def project(u, p):
                pe.wait_ge(gelu_done, (u + 1) * HT)
                pe.wait_ge(o_raw_ready, u + ONE)
                for c in range(2):
                    for t in range(HT):
                        mm = nc.tensor.matmul(ps_o[:, c * BANK:(c + 1) * BANK], w2_sb[:, t, :],
                                              h_sb[:, p, t, c * BANK:(c + 1) * BANK],
                                              start=(t == 0), stop=(t == HT - 1))
                mm.then_inc(o_psum_ready, 1)

            hidden(0, 0, 0, 0)
            pe.wait_ge(hbias_ready, 1)

            def step(i, scan, scale, trans, last):
                for r in range(2):
                    b = i * 2 + r
                    for p in range(UPB):
                        u = b * UPB + p
                        if p == 0:
                            hidden(u + 1, b, r, 1)
                        elif not (last and r == 1):
                            hidden(u + 1, b + 1, 1 - r, 0)
                        project(u, p)

            run_steps(pe, step)

            pe.wait_ge(gelu_done, B * UPB * HT)
            for r in range(2):
                pe.wait_ge(w_transposed[r], NT // 2 * 16 + DMA)

            def step2(i, last):
                for r in range(2):
                    b = i * 2 + r
                    first = isinstance(b, int) and b == 0
                    if not first:
                        pe.wait_ge(qT_loaded[r], (i + r) * 16 + DMA)
                    for n in range(NC):
                        pe.wait_ge(y_ready, b * NC + n + 1)
                        for k in range(KT):
                            if first and n == 0 and k % (KT // CUTS) == 0:
                                pe.wait_ge(qT_cut[k // (KT // CUTS)], 16)
                            mm = nc.tensor.matmul(ps_y[n], qT[:, r, k, :], wqT[:, k, n * BANK:(n + 1) * BANK],
                                                  start=(k == 0), stop=(k == KT - 1))
                        mm.then_inc(y_psum, 1)

            step2(0, False)
            with pe.Fori(1, STEPS - 1) as i:
                step2(i, False)
            step2(STEPS - 1, True)


_INS = ["x", "itok_B_0_7", "itok_B_2182_4065", "_lenS", "L0_cond_W_sess", "L0_cond_b_sess", "L0_cond_W2",
        "L0_cond_b2", "L0_ffn_weight", "L0_ffn_bias"]


def kernel(**inputs):
    import concourse.bacc as bacc
    from concourse.bass_utils import run_bass_kernel_spmd

    nc = bacc.Bacc("TRN2", target_bir_lowering=False, num_devices=1)
    arrays, args = {}, []
    for name in _INS:
        a = np.ascontiguousarray(inputs[name])
        arrays[f"in_{name}"] = a
        args.append(nc.dram_tensor(f"in_{name}", a.shape, mybir.dt.from_np(a.dtype), kind="ExternalInput").ap())
    shape = inputs["x"].shape
    out = nc.dram_tensor("out", shape, mybir.dt.float32, kind="ExternalOutput").ap()
    masked_out = nc.dram_tensor("masked_out", shape, mybir.dt.float32, kind="Internal").ap()
    adaln_ffn(nc, *args, out, masked_out)
    return run_bass_kernel_spmd(nc, [arrays], core_ids=[0]).results[0]["out"]
```

```python
import concourse.bass as bass
from concourse import mybir
from contextlib import ExitStack
import numpy as np


def adaln_ffn(nc, x, ids, lens, counts, w_sess, b_sess, w2, b2, weight, bias, out, masked_out):
    fp32, bf16, fp8, i32 = mybir.dt.float32, mybir.dt.bfloat16, mybir.dt.float8e5, mybir.dt.int32
    fp32r = mybir.dt.float32r
    u16 = mybir.dt.uint16
    ALU, ACT, AX = mybir.AluOpType, mybir.ActivationFunctionType, mybir.AxisListType
    ds = bass.ds

    P = 128
    B, C, T = x.shape
    NSESS, _, HID = w_sess.shape
    HT = HID // P
    F = weight.shape[0]
    BANK = 512
    UNIT = 2 * BANK
    UPB = T // UNIT
    NT = F // P
    KT = T // P
    NC = F // BANK
    STEPS = B // 2
    E4M3_MAX, E5M2_MAX, EPS = 448.0, 57344.0, 1e-12
    EXPONENT = 0x7F80
    E4M3_MIN_NORMAL = 2.0 ** -6
    ROUND_AT = 1.5 * 2.0 ** 20
    assert C == P and UPB == 2 and NT == KT and B == 2 * NT

    SLOTS = 3
    SCAN = (NT - 1) // SLOTS
    QUANT = SCAN + NT // 2
    SEGMENTS = [(0, 1, True, False, False), (1, SCAN, True, False, False), (SCAN, SCAN + 1, False, True, False),
                (SCAN + 1, QUANT, False, True, True), (QUANT, QUANT + 1, False, False, True),
                (QUANT + 1, STEPS - 1, False, False, False), (STEPS - 1, STEPS, False, False, False)]
    assert NT % SLOTS == 1 and QUANT + 1 < STEPS
    CUTS = 4
    CUT = [slice(k * T // CUTS, (k + 1) * T // CUTS) for k in range(CUTS)]
    WHOLE, HALVES = [slice(0, UNIT)], [slice(0, BANK), slice(BANK, UNIT)]
    WARM_START, WARM_MIDDLE = 2, 24
    EARLY_END = SCAN * 2 * UPB + 1
    LATE, LATE_END = (QUANT + 1) * 2 * UPB, B * UPB - 1

    def in_parts(u, scan):
        if isinstance(u, int):
            return 0 if u >= LATE_END else UNIT if u < EARLY_END or u >= LATE else BANK
        return UNIT if scan else BANK

    FREE4 = 4
    ONE, DMA = 1, 16

    with ExitStack() as ctx:
        def sb(name, shape, dt):
            return ctx.enter_context(nc.sbuf_tensor(name, shape, dt))

        def sem(name):
            return ctx.enter_context(nc.semaphore(name))

        ids_i = sb("ids_i", [P, B], i32)
        counts_i = sb("counts_i", [P, B], i32)
        lens_i = sb("lens_i", [P, B], i32)
        ids_f = sb("ids_f", [P, B], fp32)
        counts_f = sb("counts_f", [P, B], fp32)
        lens_f = sb("lens_f", [P, UPB, B], fp32)
        chan = sb("chan", [P, 1], fp32)
        time = sb("time", [P, UNIT], fp32)
        onehot = sb("onehot", [NSESS, B], fp32)
        cmask = sb("cmask", [P, B], fp32)
        bs_sb = sb("bs_sb", [NSESS, HID], fp32)
        hbias = sb("hbias", [P, HT, B], fp32)
        w2_sb = sb("w2_sb", [P, HT, P], fp32)
        w2h = sb("w2h", [P, P], fp32r)
        w2l = sb("w2l", [P, P], fp32r)
        b2_sb = sb("b2_sb", [P, 1], fp32)
        unread = sb("unread", [P, 1], fp32)
        ident = sb("ident", [P, P], fp8)
        wqT = sb("wqT", [P, KT, F], bf16)
        w_max = sb("w_max", [P, NT], fp32)
        o_max = sb("o_max", [P, B * UPB + 1], fp32)
        scales = sb("scales", [P, 13], fp32)
        w_pmax, w_amax, w_clip, w_rec, w_scale, w_inv = (scales[:, k:k + 1] for k in range(6))
        o_pmax, o_amax, o_clip, o_rec, o_scale, o_inv, y_scale = (scales[:, k:k + 1] for k in range(6, 13))

        x_sb = sb("x_sb", [P, 2, T], fp32)
        wraw = sb("wraw", [P, 2, HID], fp32)
        wh = sb("wh", [P, 2, HID], fp32r)
        wl = sb("wl", [P, 2, HID], fp32r)
        xh = sb("xh", [P, 2, UNIT], fp32r)
        xl = sb("xl", [P, 2, UNIT], fp32r)
        h_sb = sb("h_sb", [P, 2, HT, UNIT], fp32)
        hh = sb("hh", [P, 2, UNIT], fp32r)
        hl = sb("hl", [P, 2, UNIT], fp32r)
        o_sb = sb("o_sb", [P, 2, T], fp32)
        wt = sb("wt", [P, 2, T], fp32)
        ws = sb("ws", [P, 2, T], fp32)
        wp = sb("wp", [P, 2, T], bf16)
        wq = sb("wq", [P, 2, T], bf16)
        qT = ws[:, 0, :].bitcast(bf16).rearrange("p (r k t) -> p r k t", r=2, k=KT)
        bias_sb = ws[:, 1, :]
        qb = x_sb[:, 0, :].bitcast(bf16).rearrange("p (r t) -> p r t", r=2)
        q8 = x_sb[:, 1, 0:T // 2].bitcast(fp8).rearrange("p (r t) -> p r t", r=2)
        x2 = (wp[:, :, :].rearrange("p a t -> p (a t)").bitcast(fp32),
              h_sb[:, 0, :, :].rearrange("p a n -> p (a n)"))
        o_in, y_sb = wt, o_sb
        scan_sb = (wt[:, 0, :], wt[:, 1, :], ws[:, 0, :], ws[:, 1, :])

        ps_h = ctx.enter_context(nc.psum_tensor("ps_h", [P, HT, UNIT], fp32))
        ps_o = ctx.enter_context(nc.psum_tensor("ps_o", [P, 2, UNIT], fp32))
        ps_q = ps_o[:, :, :].rearrange("p a n -> p (a n)")
        ps_y = [ps_h[:, n // 2, n % 2 * BANK:(n % 2 + 1) * BANK] for n in range(NC)]

        params_loaded = sem("params_loaded")
        bs_loaded = sem("bs_loaded")
        ids_loaded = sem("ids_loaded")
        bias_loaded = sem("bias_loaded")
        iota_ready = sem("iota_ready")
        const_step = sem("const_step")
        onehot_ready = sem("onehot_ready")
        hbias_psum = sem("hbias_psum")
        hbias_ready = sem("hbias_ready")
        x_loaded = [sem(f"x_loaded{r}") for r in range(2)]
        x_first = [sem(f"x_first{p}") for p in range(UPB)]
        wraw_loaded = [sem(f"wraw_loaded{r}") for r in range(2)]
        wh_ready = sem("wh_ready")
        wl_ready = sem("wl_ready")
        xh_ready = sem("xh_ready")
        xl_ready = sem("xl_ready")
        h_psum_ready = sem("h_psum_ready")
        gelu_done = sem("gelu_done")
        h_first_done = sem("h_first_done")
        w2_split = sem("w2_split")
        hl_ready = sem("hl_ready")
        o_psum_ready = sem("o_psum_ready")
        o_unmasked_ready = sem("o_unmasked_ready")
        o_masked = sem("o_masked")
        o_scanned = sem("o_scanned")
        o_stored = [sem(f"o_stored{r}") for r in range(2)]
        scan_loaded = [sem(f"scan_loaded{k}") for k in range(SLOTS + 1)]
        wt_loaded = [sem(f"wt_loaded{r}") for r in range(2)]
        wt_scanned = sem("wt_scanned")
        scale_step = sem("scale_step")
        w_pmax_ready = sem("w_pmax_ready")
        w_amax_ready = sem("w_amax_ready")
        w_scale_ready = sem("w_scale_ready")
        w_scaled = sem("w_scaled")
        w_exponent = sem("w_exponent")
        w_round_ready = sem("w_round_ready")
        w_added = sem("w_added")
        w_rounded = sem("w_rounded")
        w_transposed = [sem(f"w_transposed{r}") for r in range(2)]
        o_pmax_ready = sem("o_pmax_ready")
        o_amax_ready = sem("o_amax_ready")
        o_in_loaded = [sem(f"o_in_loaded{r}") for r in range(2)]
        x2_loaded = [sem(f"x2_loaded{r}") for r in range(2)]
        q_widened = sem("q_widened")
        q_turned = sem("q_turned")
        qT_loaded = [sem(f"qT_loaded{r}") for r in range(2)]
        xb_ready = sem("xb_ready")
        q_ready = sem("q_ready")
        y_psum = sem("y_psum")
        y_ready = sem("y_ready")
        y_chunk_stored = [sem(f"y_chunk_stored{n}") for n in range(NC)]
        y_stored = [sem(f"y_stored{r}") for r in range(2)]

        gelu_turn = sem("gelu_turn")
        q_turn = sem("q_turn")
        widen_turn = sem("widen_turn")
        load_turn = sem("load_turn")
        transpose_turn = sem("transpose_turn")
        identity_turn = sem("identity_turn")

        block = ctx.enter_context(nc.Block())

        def run_steps(eng, step):
            for first, end, scan, scale, trans in SEGMENTS:
                if end - first == 1:
                    step(first, scan, scale, trans, end == STEPS)
                else:
                    with eng.Fori(first, end) as i:
                        step(i, scan, scale, trans, False)

        def split_h_rest(eng, u, p, parts):
            eng.wait_ge(h_first_done, u + 1)
            eng.wait_ge(gelu_done, u * HT + 1)
            if not isinstance(u, int) or u > 0:
                eng.wait_ge(hl_ready, u)
            eng.tensor_tensor(hl[:, p, 0:parts], h_sb[:, p, 0, 0:parts], hh[:, p, 0:parts].bitcast(fp32),
                              ALU.subtract).then_inc(hl_ready, 1)

        @block.sync
        def _(sp):
            for r in range(2):
                for count in (o_stored[r], y_stored[r], w_transposed[r], qT_loaded[r]):
                    sp.sem_inc(count, DMA)

            def load_x(b, r):
                sp.dma_start(x_sb[:, r, :], x[ds(b, 1), :, :].rearrange("a c t -> (a c) t"))\
                  .then_inc(x_loaded[r], 16)

            def load_session_weight(b, r):
                sid = sp.value_load(ids_i[0:1, ds(b, 1)], min_val=0, max_val=NSESS - 1)
                sp.dma_start(wraw[:, r, :], w_sess[ds(sid, 1), :, :].rearrange("a c h -> (a c) h"))\
                  .then_inc(wraw_loaded[r], 16)

            def load_weight(tile, buffer, loaded):
                sp.dma_start(buffer, weight[ds(tile * P, P), :]).then_inc(loaded, 16)

            for dst, src in ((ids_i, ids), (counts_i, counts), (lens_i, lens)):
                sp.dma_start(dst[:, :], src.partition_broadcast(P)).then_inc(ids_loaded, 16)
            sp.dma_start(bs_sb[:, :], b_sess).then_inc(bs_loaded, 16)

            def load_x_part(p):
                cols = slice(p * UNIT, (p + 1) * UNIT)
                sp.dma_start(x_sb[:, 0, cols], x[0, :, cols]).then_inc(x_first[p], 16)

            load_x_part(0)
            sp.wait_ge(ids_loaded, 48)
            load_session_weight(0, 0)
            load_x_part(1)
            sp.dma_start(w2_sb[:, :, :], w2.rearrange("(j p) s -> p j s", p=P)).then_inc(params_loaded, 16)
            sp.dma_start(b2_sb[:, :], b2.rearrange("(p a) -> p a", a=1)).then_inc(params_loaded, 16)
            load_session_weight(1, 1)
            load_x(1, 1)
            load_weight(NT - 1, scan_sb[SLOTS], scan_loaded[SLOTS])
            sp.wait_ge(wl_ready, 1)
            load_session_weight(2, 0)
            sp.wait_ge(xl_ready, UPB)
            load_x(2, 0)

            def load_o(b, r):
                sp.dma_start(o_in[:, r, :], masked_out[ds(b, 1), :, :].rearrange("a s t -> (a s) t"))\
                  .then_inc(o_in_loaded[r], 16)

            def load_x_again(b, r):
                sp.dma_start(x2[r], x[ds(b, 1), :, :].rearrange("a c t -> (a c) t"))\
                  .then_inc(x2_loaded[r], 16)

            def store_o(b, r):
                sp.dma_start(masked_out[ds(b, 1), :, :].rearrange("a s t -> (a s) t"), o_sb[:, r, :])\
                  .then_inc(o_stored[r], 16)

            def step(i, scan, scale, trans, last):
                if last:
                    sp.wait_ge(w_rounded, NT + ONE)
                    for r in range(2):
                        load_o(r, r)
                    load_x_again(0, 0)
                    sp.dma_start(bias_sb, bias.partition_broadcast(P)).then_inc(bias_loaded, 16)
                for r in range(2):
                    b = i * 2 + r
                    if scan:
                        for k in ((0, 1), (2,))[r]:
                            if not isinstance(i, int):
                                sp.wait_ge(wt_scanned, i * SLOTS + k - 1)
                            load_weight(i * SLOTS + k, scan_sb[k], scan_loaded[k])
                    if scale:
                        n = b - 2 * SCAN
                        sp.wait_ge(wt_scanned, NT)
                        if not isinstance(n, int):
                            sp.wait_ge(w_scaled, (n - 1) * UPB)
                        load_weight(n, wt[:, r, :], wt_loaded[r])
                    if not isinstance(b, int) or b + 3 < B:
                        sp.wait_ge(wl_ready, b + 2)
                        sp.sem_inc(load_turn, 1)
                        load_session_weight(b + 3, 1 - r)
                        sp.wait_ge(xl_ready, (b + 2) * UPB)
                        load_x(b + 3, 1 - r)
                    if not (last and r == 1):
                        sp.wait_ge(o_masked, (b + 1) * UPB)
                        store_o(b, r)
                    if trans:
                        n = b - 2 * SCAN - 2
                        sp.wait_ge(w_rounded, n + 1 + ONE)
                        sp.sem_inc(transpose_turn, 1)
                        sp.dma_start_transpose(wqT[:, :, ds(n * P, P)], wq[:, r, :]).then_inc(w_transposed[r], 16)

            run_steps(sp, step)

            sp.wait_ge(o_psum_ready, B * UPB - 1 + ONE)
            load_x_again(1, 1)
            sp.wait_ge(o_masked, B * UPB + 1)
            store_o(B - 1, 1)
            for r in range(2):
                sp.wait_ge(o_stored[r], 16 * STEPS + DMA)

            def step2(i, last):
                for r in range(2):
                    b = i * 2 + r
                    if not last:
                        sp.wait_ge(q_ready, b + CUTS)
                        load_o(b + 2, r)
                    if not (last and r == 1):
                        sp.wait_ge(y_psum, b * NC + ONE)
                        sp.sem_inc(load_turn, 1)
                        sp.wait_ge(q_widened, b + 1 + CUTS + ONE)
                        sp.sem_inc(transpose_turn, 1)
                        sp.dma_start_transpose(qT[:, 1 - r, :, :], qb[:, 1 - r, :])\
                          .then_inc(qT_loaded[1 - r], 16)
                    if last and r == 1:
                        for n in range(NC):
                            cols = slice(n * BANK, (n + 1) * BANK)
                            sp.wait_ge(y_ready, b * NC + n + 1 + FREE4)
                            sp.dma_start(out[b, :, cols], y_sb[:, r, cols]).then_inc(y_chunk_stored[n], 16)
                        continue
                    sp.wait_ge(y_ready, (b + 1) * NC + FREE4)
                    sp.dma_start(out[ds(b, 1), :, :].rearrange("a s n -> (a s) n"), y_sb[:, r, :])\
                      .then_inc(y_stored[r], 16)
                    if not last:
                        load_x_again(b + 2, r)

            with sp.Fori(0, STEPS - 1) as i:
                step2(i, False)
            step2(STEPS - 1, True)
            for r in range(2):
                sp.wait_ge(y_stored[r], 16 * (STEPS - r) + DMA)
            for n in range(NC):
                sp.wait_ge(y_chunk_stored[n], 16)

        @block.gpsimd
        def _(pool):
            pool.sem_inc(w_rounded, ONE)
            pool.iota(time[:, :], pattern=[[1, UNIT]], base=0, channel_multiplier=0,
                      allow_small_or_imprecise_dtypes=True).then_inc(iota_ready, 1)
            pool.iota(chan[:, :], pattern=[[0, 1]], base=0, channel_multiplier=1,
                      allow_small_or_imprecise_dtypes=True).then_inc(iota_ready, 1)

            def split_x_rest(u, r, p):
                pool.wait_ge(xh_ready, u + 1)
                pool.tensor_tensor(xl[:, p, :], x_sb[:, r, p * UNIT:(p + 1) * UNIT], xh[:, p, :].bitcast(fp32),
                                   ALU.subtract).then_inc(xl_ready, 1)

            split_h_rest(pool, 0, 0, in_parts(0, True))

            def step(i, scan, scale, trans, last):
                for r in range(2):
                    b = i * 2 + r
                    n = b - 2 * SCAN - 2
                    v, c = ws[:, r, :], wp[:, r, :]
                    for p in range(UPB):
                        if scan or not trans and scale:
                            split_x_rest((b + 1) * UPB + p, 1 - r, p)
                        u = b * UPB + p
                        if in_parts(u + 1, scan) == UNIT or in_parts(u + 1, scan) and p == 1:
                            split_h_rest(pool, u + 1, 1 - p, in_parts(u + 1, scan))
                        if not trans and scale and r == 0 and p == 0:
                            pool.wait_ge(w_pmax_ready, 1)
                            pool.partition_all_reduce(w_amax, w_pmax, P, bass.bass_isa.ReduceOp.max)\
                                .then_inc(w_amax_ready, 1)
                        if trans and p == 0:
                            pool.wait_ge(w_round_ready, n + 1)
                            pool.tensor_tensor(v, v, c, ALU.add).then_inc(w_added, 1)
                        if trans and p == 1:
                            pool.wait_ge(w_added, n + 1)
                            pool.wait_ge(w_transposed[r], (i - SCAN - 1) * 16 + DMA)
                            pool.tensor_tensor(wq[:, r, :], v, c, ALU.subtract).then_inc(w_rounded, 1)

            run_steps(pool, step)

            pool.wait_ge(o_pmax_ready, 1)
            pool.partition_all_reduce(o_amax, o_pmax, P, bass.bass_isa.ReduceOp.max).then_inc(o_amax_ready, 1)
            pool.wait_ge(bias_loaded, 16)
            with pool.Fori(0, STEPS) as i:
                for r in range(2):
                    pool.wait_ge(x2_loaded[r], (i + 1) * 16)
                    pool.tensor_tensor(x2[r], x2[r], bias_sb, ALU.add).then_inc(xb_ready, 1)

        @block.scalar
        def _(act):
            act.sem_inc(q_widened, ONE)
            act.sem_inc(o_unmasked_ready, ONE)

            def gelu(u, b, ub, parts):
                for t in range(HT):
                    act.wait_ge(h_psum_ready, u * HT + t + 1 + ONE)
                    act.sem_inc(gelu_turn, 1)
                    first = parts and t == 0
                    act.activation(h_sb[:, ub, t, :], ps_h[:, t, :], ACT.Gelu, bias=hbias[:, t, ds(b, 1)])\
                       .then_inc(h_first_done if first else gelu_done, 1)
                    if first:
                        act.activation(hh[:, ub, 0:parts], ps_h[:, t, 0:parts], ACT.Gelu,
                                       bias=hbias[:, t, ds(b, 1)]).then_inc(gelu_done, 1)

            def add_b2(u, i, r, p, last):
                act.wait_ge(o_stored[r], i * 16 + DMA)
                act.wait_ge(o_scanned, u + 1)
                for k, cols in enumerate(HALVES if last else WHOLE):
                    act.wait_ge(o_psum_ready, u + k + 1 + ONE)
                    act.activation(o_sb[:, r, p * UNIT + cols.start:p * UNIT + cols.stop], ps_o[:, p, cols],
                                   ACT.Identity, bias=b2_sb[:, :]).then_inc(o_unmasked_ready, 1)

            def split_x(u, r, p, loads):
                act.wait_ge(x_loaded[r], loads * 16)
                if not isinstance(u, int) or u > 1:
                    act.wait_ge(h_psum_ready, (u - 1) * HT + ONE)
                act.activation(xh[:, p, :], x_sb[:, r, p * UNIT:(p + 1) * UNIT], ACT.Copy).then_inc(xh_ready, 1)

            act.wait_ge(hbias_psum, 1)
            act.activation(hbias[:, :, :], ps_o[:, 0, 0:HT * B].rearrange("p (t b) -> p t b", t=HT), ACT.Copy)\
               .then_inc(hbias_ready, 1)
            act.wait_ge(hbias_ready, 1)
            act.activation(unread[:, :], hbias[:, 0, 0:1], ACT.Gelu)
            gelu(0, 0, 0, in_parts(0, True))
            act.wait_ge(xl_ready, UPB)

            def step(i, scan, scale, trans, last):
                for r in range(2):
                    b = i * 2 + r
                    for p in range(UPB):
                        u = b * UPB + p
                        if not (last and r == 1):
                            split_x((b + 1) * UPB + p, 1 - r, p, i + 1)
                        if not (last and r == 1 and p == 1):
                            act.wait_ge(o_psum_ready, u + ONE)
                            gelu(u + 1, b + (p + 1) // UPB, (p + 1) % 2, in_parts(u + 1, scan))
                        n, cols = b - 2 * SCAN - 1, slice(p * UNIT, (p + 1) * UNIT)
                        if (scale or trans) and (not isinstance(n, int) or 0 <= n < NT):
                            if isinstance(n, int) and n == 0:
                                act.wait_ge(w_scale_ready, 1)
                            else:
                                act.wait_ge(w_rounded, n - 1 + ONE)
                            act.wait_ge(wt_loaded[1 - r], (i + r - SCAN) * 16)
                            act.activation(ws[:, 1 - r, cols], wt[:, 1 - r, cols], ACT.Copy, scale=w_scale)\
                               .then_inc(w_scaled, 1)
                        add_b2(u, i, r, p, last and r == 1 and p == 1)

            run_steps(act, step)

            for k in range(CUTS):
                act.wait_ge(q_turned, k + 1)
                act.activation(qT[:, 0, k * KT // CUTS:(k + 1) * KT // CUTS, :],
                               ps_q[:, CUT[k]].rearrange("p (k t) -> p k t", t=P), ACT.Copy).then_inc(q_widened, 1)

            def widen(b, r, uses):
                act.wait_ge(q_ready, b + CUTS)
                act.wait_ge(qT_loaded[r], uses * 16 + DMA)
                act.sem_inc(widen_turn, 1)
                act.activation(qb[:, r, :], q8[:, r, :], ACT.Copy).then_inc(q_widened, 1)

            widen(1, 1, 0)
            with act.Fori(0, STEPS - 1) as i:
                widen(i * 2 + 2, 0, i)
                widen(i * 2 + 3, 1, i + 1)

        @block.vector
        def _(dve):
            dve.sem_inc(y_ready, FREE4)
            dve.sem_inc(o_scanned, FREE4)
            dve.wait_ge(ids_loaded, 48)
            dve.tensor_copy(ids_f[:, :], ids_i[:, :]).then_inc(const_step, 1)
            dve.tensor_copy(counts_f[:, :], counts_i[:, :]).then_inc(const_step, 1)
            for p in range(UPB):
                dve.tensor_scalar(lens_f[:, p, :], lens_i[:, :], float(-p * UNIT), None, ALU.add)\
                   .then_inc(const_step, 1)
            dve.wait_ge(iota_ready, 2)
            dve.wait_ge(const_step, 4)
            dve.tensor_scalar(onehot[:, :], ids_f[0:NSESS, :], chan[0:NSESS, :], None, ALU.is_equal)\
               .then_inc(onehot_ready, 1)
            dve.tensor_scalar(cmask[:, :], counts_f[:, :], chan[:, :], None, ALU.is_gt).then_inc(const_step, 1)
            dve.wait_ge(const_step, 5)

            def mask_weight(b, r, loads):
                dve.wait_ge(wraw_loaded[r], loads * 16)
                mask = cmask[:, ds(b, 1)]
                dve.tensor_scalar(wh[:, r, :], wraw[:, r, :], mask, None, ALU.mult).then_inc(wh_ready, 1)
                dve.wait_ge(wh_ready, b + 1)
                dve.scalar_tensor_tensor(wl[:, r, :], wraw[:, r, :], mask, wh[:, r, :].bitcast(fp32),
                                         ALU.mult, ALU.subtract).then_inc(wl_ready, 1)

            def split_x_rest(u, r, p):
                dve.wait_ge(xh_ready, u + 1)
                if not isinstance(u, int) or u > 0:
                    dve.wait_ge(xl_ready, u)
                dve.tensor_tensor(xl[:, p, :], x_sb[:, r, p * UNIT:(p + 1) * UNIT], xh[:, p, :].bitcast(fp32),
                                  ALU.subtract).then_inc(xl_ready, 1)

            dve.tensor_scalar(ident[:, :], time[:, 0:P], chan[:, :], None, ALU.is_equal, saturate=False)\
               .then_inc(const_step, 1)
            mask_weight(0, 0, 1)
            for p in range(UPB):
                dve.wait_ge(x_first[p], 16)
                dve.tensor_copy(xh[:, p, :], x_sb[:, 0, p * UNIT:(p + 1) * UNIT]).then_inc(xh_ready, 1)
                split_x_rest(p, 0, p)
            mask_weight(1, 1, 1)
            dve.wait_ge(params_loaded, 32)
            dve.tensor_copy(w2h[:, :], w2_sb[:, 0, :]).then_inc(w2_split, 1)
            dve.wait_ge(w2_split, 1)
            dve.tensor_tensor(w2l[:, :], w2_sb[:, 0, :], w2h[:, :].bitcast(fp32), ALU.subtract)\
               .then_inc(w2_split, 1)

            def weight_maximum():
                dve.wait_ge(wt_scanned, NT)
                dve.tensor_reduce(w_pmax, w_max[:, :], AX.X, ALU.max).then_inc(w_pmax_ready, 1)

            def weight_scale():
                dve.wait_ge(w_amax_ready, 1)
                dve.tensor_scalar(w_clip, w_amax, EPS, None, ALU.max).then_inc(scale_step, 1)
                dve.wait_ge(scale_step, 1)
                dve.reciprocal(w_rec, w_clip).then_inc(scale_step, 1)
                dve.wait_ge(scale_step, 2)
                dve.tensor_scalar(w_scale, w_rec, E4M3_MAX, None, ALU.mult).then_inc(w_scale_ready, 1)
                dve.wait_ge(w_scale_ready, 1)
                dve.reciprocal(w_inv, w_scale).then_inc(scale_step, 1)

            def step(i, scan, scale, trans, last):
                for r in range(2):
                    b = i * 2 + r
                    for p in range(UPB):
                        u = b * UPB + p
                        splits = trans or not (scan or scale) or scale and r == p == 1
                        if in_parts(u + 1, scan) == BANK and p == 0:
                            split_h_rest(dve, u + 1, 1, BANK)
                        if scale and isinstance(i, int) and r == 0:
                            if p == 0:
                                weight_maximum()
                            else:
                                weight_scale()
                        n = b - 2 * SCAN - 1
                        if (scale or trans) and (not isinstance(n, int) or 0 <= n < NT) and p == 1:
                            v = ws[:, 1 - r, :].bitcast(u16).rearrange("p (t k) -> p t k", k=2)[:, :, 1]
                            c = wp[:, 1 - r, :]
                            dve.wait_ge(w_scaled, (n + 1) * UPB)
                            dve.tensor_scalar(c.bitcast(u16), v, EXPONENT, None,
                                              ALU.bitwise_and).then_inc(w_exponent, 1)
                            dve.wait_ge(w_exponent, n + 1)
                            dve.tensor_scalar(c, c, E4M3_MIN_NORMAL, ROUND_AT, ALU.max, ALU.mult)\
                               .then_inc(w_round_ready, 1)
                        for k, cols in enumerate(HALVES if last and r == 1 and p == 1 else WHOLE):
                            part = o_sb[:, r, p * UNIT + cols.start:p * UNIT + cols.stop]
                            dve.wait_ge(o_unmasked_ready, u + k + 1 + ONE)
                            dve.scalar_tensor_tensor(part, time[:, cols], lens_f[:, p, ds(b, 1)],
                                                     part, ALU.is_lt, ALU.mult).then_inc(o_masked, 1)
                            if splits and not (isinstance(u, int) and u + 3 >= B * UPB):
                                split_x_rest(u + 3, 1 - r if p == 0 else r, 1 - p)
                            dve.wait_ge(o_masked, u + k + 1)
                            dve.tensor_reduce(o_max[:, ds(u + k, 1)], part, AX.X, ALU.max,
                                              apply_absolute_value=True).then_inc(o_scanned, 1)
                        if p == 0 and not last:
                            dve.wait_ge(h_psum_ready, (b + 1) * UPB * HT + ONE)
                            mask_weight(b + 2, r, i + 2)
                        k = 2 * r + p - 1
                        if scan and (k >= 0 or isinstance(i, int)):
                            n, k, loads = (i * SLOTS + k, k, i + 1) if k >= 0 else (NT - 1, SLOTS, 1)
                            dve.wait_ge(scan_loaded[k], loads * 16)
                            dve.tensor_reduce(w_max[:, ds(n, 1)], scan_sb[k], AX.X, ALU.max,
                                              apply_absolute_value=True).then_inc(wt_scanned, 1)

            run_steps(dve, step)

            dve.wait_ge(o_scanned, B * UPB + 1 + FREE4)
            dve.tensor_reduce(o_pmax, o_max[:, :], AX.X, ALU.max).then_inc(o_pmax_ready, 1)
            dve.wait_ge(o_amax_ready, 1)
            dve.tensor_scalar(o_clip, o_amax, EPS, None, ALU.max).then_inc(scale_step, 1)
            dve.wait_ge(scale_step, 4)
            dve.reciprocal(o_rec, o_clip).then_inc(scale_step, 1)
            dve.wait_ge(scale_step, 5)
            dve.tensor_scalar(o_scale, o_rec, E5M2_MAX, None, ALU.mult).then_inc(scale_step, 1)
            dve.wait_ge(scale_step, 6)

            def quantize(r, loads, first, cols):
                if first:
                    dve.wait_ge(o_in_loaded[r], loads * 16)
                dve.sem_inc(q_turn, 1)
                dve.tensor_scalar(q8[:, r, cols], o_in[:, r, cols], o_scale, None, ALU.mult, saturate=False)\
                   .then_inc(q_ready, 1)

            for k in range(CUTS):
                quantize(0, 1, k == 0, CUT[k])
            dve.reciprocal(o_inv, o_scale).then_inc(scale_step, 1)
            dve.wait_ge(scale_step, 7)
            dve.tensor_tensor(y_scale, o_inv, w_inv, ALU.mult).then_inc(scale_step, 1)
            dve.wait_ge(scale_step, 8)

            def step2(i, last):
                for r in range(2):
                    b = i * 2 + r
                    if not (last and r == 1):
                        dve.wait_ge(q_widened, b + CUTS - 1 + ONE)
                        quantize(1 - r, i + 1 + r, True, slice(0, T))
                    dve.wait_ge(xb_ready, b + 1)
                    dve.wait_ge(y_stored[r], i * 16 + DMA)
                    for n in range(NC):
                        cols = slice(n * BANK, (n + 1) * BANK)
                        dve.wait_ge(y_psum, b * NC + n + 1 + ONE)
                        dve.scalar_tensor_tensor(y_sb[:, r, cols], ps_y[n], y_scale, x2[r][:, cols],
                                                 ALU.mult, ALU.add).then_inc(y_ready, 1)

            for r in range(2):
                dve.wait_ge(o_stored[r], 16 * STEPS + DMA)
            with dve.Fori(0, STEPS - 1) as i:
                step2(i, False)
            step2(STEPS - 1, True)

        @block.tensor
        def _(pe):
            for count in (h_psum_ready, o_psum_ready, y_psum):
                pe.sem_inc(count, ONE)

            def warm_up(count):
                for k in range(count):
                    nc.tensor.matmul(ps_o[:, 1, 0:BANK], time[:, 0:P], time[:, 0:BANK], start=True, stop=True)

            pe.wait_ge(iota_ready, 1)
            warm_up(WARM_START)
            pe.wait_ge(bs_loaded, 16)
            pe.wait_ge(onehot_ready, 1)
            for t in range(HT):
                last_mm = nc.tensor.matmul(ps_o[:, 0, t * B:(t + 1) * B], bs_sb[:, t * P:(t + 1) * P],
                                           onehot[:, :], start=True, stop=True)
            last_mm.then_inc(hbias_psum, 1)
            warm_up(WARM_START)

            def hidden(u, b, r, p):
                if p == 0:
                    pe.wait_ge(wl_ready, b + 1)
                pe.wait_ge(xh_ready, u + 1)
                for t in range(HT):
                    if not isinstance(u, int) or u > 0:
                        pe.wait_ge(gelu_done, (u - 1) * HT + t + 1)
                    rows = slice(t * P, (t + 1) * P)
                    for k, (w, xs) in enumerate(((wl, xh), (wh, xh), (wh, xl))):
                        if k == 2 and t == 0:
                            pe.wait_ge(xl_ready, u + 1)
                        for c in range(2):
                            cols = slice(c * BANK, (c + 1) * BANK)
                            mm = nc.tensor.matmul(ps_h[:, t, cols], w[:, r, rows], xs[:, p, cols],
                                                  start=(k == 0), stop=(k == 2))
                    mm.then_inc(h_psum_ready, 1)

            def project(u, p, parts, last):
                if not isinstance(u, int) or u > 1:
                    pe.wait_ge(o_unmasked_ready, u - 1 + ONE)
                split, whole = range(parts // BANK), range(parts // BANK, UNIT // BANK)
                by_tile = [(t, c) for t in range(HT) for c in range(2) if t > 0 or c in whole]
                for t, c in [(0, 0), (1, 0), (0, 1), (1, 1)] if last else by_tile:
                    pe.wait_ge(gelu_done, u * HT + t + 1)
                    mm = nc.tensor.matmul(ps_o[:, p, c * BANK:(c + 1) * BANK], w2_sb[:, t, :],
                                          h_sb[:, p, t, c * BANK:(c + 1) * BANK],
                                          start=(t == 0 or c in split), stop=(t == HT - 1 and c in whole))
                    if last and t == HT - 1:
                        mm.then_inc(o_psum_ready, 1)
                for k, (w, hs) in enumerate(() if last else ((w2l, hh), (w2h, hh), (w2h, hl))):
                    if k == 2:
                        pe.wait_ge(hl_ready, u + 1)
                    for c in split:
                        cols = slice(c * BANK, (c + 1) * BANK)
                        mm = nc.tensor.matmul(ps_o[:, p, cols], w[:, :], hs[:, p, cols],
                                              start=False, stop=(k == 2))
                if not last:
                    mm.then_inc(o_psum_ready, 1)

            hidden(0, 0, 0, 0)
            pe.wait_ge(hbias_ready, 1)
            pe.wait_ge(w2_split, 2)

            def step(i, scan, scale, trans, last):
                for r in range(2):
                    b = i * 2 + r
                    for p in range(UPB):
                        u = b * UPB + p
                        if p == 0:
                            hidden(u + 1, b, r, 1)
                        elif not (last and r == 1):
                            hidden(u + 1, b + 1, 1 - r, 0)
                        project(u, p, in_parts(u, scan), last and r == 1 and p == 1)

            run_steps(pe, step)

            pe.wait_ge(gelu_done, B * UPB * HT)
            for r in range(2):
                pe.wait_ge(w_transposed[r], NT // 2 * 16 + DMA)
            for k in range(WARM_MIDDLE):
                nc.tensor.matmul(ps_y[0], wqT[:, 0, 0:P], wqT[:, 0, 0:BANK], start=True, stop=True)
            pe.wait_ge(o_unmasked_ready, B * UPB + 1 + ONE)
            for k in range(CUTS):
                pe.wait_ge(q_ready, k + 1)
                pe.sem_inc(identity_turn, 1)
                for j in range(k * KT // CUTS, (k + 1) * KT // CUTS):
                    mm = nc.tensor.matmul(ps_q[:, j * P:(j + 1) * P], q8[:, 0, j * P:(j + 1) * P], ident[:, :],
                                          start=True, stop=True)
                mm.then_inc(q_turned, 1)

            def step2(i, last):
                for r in range(2):
                    b = i * 2 + r
                    first = isinstance(b, int) and b == 0
                    if not first:
                        pe.wait_ge(qT_loaded[r], (i + r) * 16 + DMA)
                    for n in range(NC):
                        pe.wait_ge(y_ready, b * NC + n + 1)
                        for k in range(KT):
                            if first and n == 0 and k % (KT // CUTS) == 0:
                                pe.wait_ge(q_widened, k // (KT // CUTS) + 1 + ONE)
                            mm = nc.tensor.matmul(ps_y[n], qT[:, r, k, :], wqT[:, k, n * BANK:(n + 1) * BANK],
                                                  start=(k == 0), stop=(k == KT - 1))
                        mm.then_inc(y_psum, 1)

            step2(0, False)
            with pe.Fori(1, STEPS - 1) as i:
                step2(i, False)
            step2(STEPS - 1, True)


_INS = ["x", "itok_B_0_7", "itok_B_2182_4065", "_lenS", "L0_cond_W_sess", "L0_cond_b_sess", "L0_cond_W2",
        "L0_cond_b2", "L0_ffn_weight", "L0_ffn_bias"]


def kernel(**inputs):
    import concourse.bacc as bacc
    from concourse.bass_utils import run_bass_kernel_spmd

    nc = bacc.Bacc("TRN2", target_bir_lowering=False, num_devices=1)
    arrays, args = {}, []
    for name in _INS:
        a = np.ascontiguousarray(inputs[name])
        arrays[f"in_{name}"] = a
        args.append(nc.dram_tensor(f"in_{name}", a.shape, mybir.dt.from_np(a.dtype), kind="ExternalInput").ap())
    shape = inputs["x"].shape
    out = nc.dram_tensor("out", shape, mybir.dt.float32, kind="ExternalOutput").ap()
    masked_out = nc.dram_tensor("masked_out", shape, mybir.dt.float32, kind="Internal").ap()
    adaln_ffn(nc, *args, out, masked_out)
    return run_bass_kernel_spmd(nc, [arrays], core_ids=[0]).results[0]["out"]
```
